# Optimizing a Trainium2 kernel written in Bass

```python
import numpy as np
import jax
import jax.numpy as jnp

def _softmax(x, axis=-1):
    return jax.nn.softmax(x, axis=axis)

def _gelu(x):
    return jax.nn.gelu(x, approximate=True)

def _silu(x):
    return jax.nn.silu(x)

def _sigmoid(x):
    return jax.nn.sigmoid(x)

def _layernorm(x, axis=-1, eps=1e-05):
    m = jnp.mean(x, axis=axis, keepdims=True)
    v = jnp.var(x, axis=axis, keepdims=True)
    return (x - m) / jnp.sqrt(v + eps)

def _scatter_add(tgt, idx, src, axis=0):
    return tgt.at[idx].add(src)

def _segment_sum(src, seg, n):
    return jax.ops.segment_sum(src, seg, n)
kernel_name = 'mk_adaln_d1_jaxref_r8_25ebad'

def setup_inputs(seed: int=0):
    np.random.seed(seed)
    _w = jnp.asarray

    def _L0_attn_setup():
        import jax, jax.numpy as jnp
        import numpy as np
        B, S, HID = (2, 256, 256)
        H, KV, D = (8, 2, 32)
        SW = 64
        SCALAR = 256.0
        EPS = 1e-06
        THETA = 1000000.0
        SOFTCAP = 30.0

        def _layernorm_unit(x, eps=EPS):
            x = x.astype(jnp.float32)
            mu = jnp.mean(x, axis=-1, keepdims=True)
            xc = x - mu
            var = jnp.mean(xc * xc, axis=-1, keepdims=True)
            return xc * jax.lax.rsqrt(var + eps)

        def _rope_cache(seq_len, head_dim, theta):
            inv_freq = 1.0 / theta ** (jnp.arange(0, head_dim, 2, dtype=jnp.float32) / head_dim)
            pos = jnp.arange(seq_len, dtype=jnp.float32)
            freqs = pos[:, None] * inv_freq[None, :]
            emb = jnp.concatenate([freqs, freqs], axis=-1)
            return (jnp.cos(emb), jnp.sin(emb))

        def _rotate_half(x):
            x1, x2 = jnp.split(x, 2, axis=-1)
            return jnp.concatenate([-x2, x1], axis=-1)
        key = jax.random.key(seed)
        ks = jax.random.split(key, 5)
        sc = 0.02
        return {'hidden_states': jax.random.normal(ks[0], (B, S, HID), dtype=jnp.float32), 'Wq': jax.random.normal(ks[1], (H * D, HID), dtype=jnp.float32) * sc, 'Wk': jax.random.normal(ks[2], (KV * D, HID), dtype=jnp.float32) * sc, 'Wv': jax.random.normal(ks[3], (KV * D, HID), dtype=jnp.float32) * sc, 'Wo': jax.random.normal(ks[4], (HID, HID), dtype=jnp.float32) * sc}
    _L0_attn_in = _L0_attn_setup()

    def _L0_ffn_setup():
        import jax, jax.numpy as jnp
        import numpy as np
        DIM = 256
        INTER = 176
        E = 16
        TOPK = 4
        G = 4
        TOPK_G = 2
        N_SHARED = 2
        ROUTE_SCALE = 1.0
        INIT_STD = 0.02
        B, S = (1, 256)
        key = jax.random.key(seed)
        ks = jax.random.split(key, 9)
        std = INIT_STD
        x = jax.random.normal(ks[0], (B, S, DIM), jnp.float32)
        gate_w = jax.random.normal(ks[1], (E, DIM), jnp.float32) * std
        expert_bias = jnp.zeros((E,), jnp.float32)
        w1 = jax.random.normal(ks[2], (E, DIM, INTER), jnp.float32) * std
        w3 = jax.random.normal(ks[3], (E, DIM, INTER), jnp.float32) * std
        w2 = jax.random.normal(ks[4], (E, INTER, DIM), jnp.float32) * std
        sh = N_SHARED * INTER
        sw1 = jax.random.normal(ks[5], (DIM, sh), jnp.float32) * std
        sw3 = jax.random.normal(ks[6], (DIM, sh), jnp.float32) * std
        sw2 = jax.random.normal(ks[7], (sh, DIM), jnp.float32) * std
        return {'x': x, 'gate_w': gate_w, 'expert_bias': expert_bias, 'w1': w1, 'w2': w2, 'w3': w3, 'sw1': sw1, 'sw2': sw2, 'sw3': sw3}
    _L0_ffn_in = _L0_ffn_setup()
    _L0_c = _w((lambda *s: np.random.randn(*s).astype(np.float32) * 0.05)(8, 256))
    _L0_wmod = _w((lambda *s: np.random.randn(*s).astype(np.float32) * 0.05)(256, 6 * 256) * 256 ** (-0.5))
    _d = {'L0_attn_hidden_states': _L0_attn_in['hidden_states'], 'L0_attn_Wq': _L0_attn_in['Wq'], 'L0_attn_Wk': _L0_attn_in['Wk'], 'L0_attn_Wv': _L0_attn_in['Wv'], 'L0_attn_Wo': _L0_attn_in['Wo'], 'L0_ffn_gate_w': _L0_ffn_in['gate_w'], 'L0_ffn_expert_bias': _L0_ffn_in['expert_bias'], 'L0_ffn_w1': _L0_ffn_in['w1'], 'L0_ffn_w2': _L0_ffn_in['w2'], 'L0_ffn_w3': _L0_ffn_in['w3'], 'L0_ffn_sw1': _L0_ffn_in['sw1'], 'L0_ffn_sw2': _L0_ffn_in['sw2'], 'L0_ffn_sw3': _L0_ffn_in['sw3'], 'L0_c': _L0_c, 'L0_wmod': _L0_wmod}
    _x0 = _d['L0_attn_hidden_states']
    _d['L0_attn_hidden_states'] = jax.random.normal(jax.random.fold_in(jax.random.key(seed), 1), (8, 256, 256), dtype=_x0.dtype)
    del _x0
    return _d

def reference(L0_attn_hidden_states, L0_attn_Wq, L0_attn_Wk, L0_attn_Wv, L0_attn_Wo, L0_ffn_gate_w, L0_ffn_expert_bias, L0_ffn_w1, L0_ffn_w2, L0_ffn_w3, L0_ffn_sw1, L0_ffn_sw2, L0_ffn_sw3, L0_c, L0_wmod):

    def _L0_attn_ref(hidden_states, Wq, Wk, Wv, Wo):
        import jax, jax.numpy as jnp
        import numpy as np
        B, S, HID = (2, 256, 256)
        H, KV, D = (8, 2, 32)
        SW = 64
        SCALAR = 256.0
        EPS = 1e-06
        THETA = 1000000.0
        SOFTCAP = 30.0

        def _layernorm_unit(x, eps=EPS):
            x = x.astype(jnp.float32)
            mu = jnp.mean(x, axis=-1, keepdims=True)
            xc = x - mu
            var = jnp.mean(xc * xc, axis=-1, keepdims=True)
            return xc * jax.lax.rsqrt(var + eps)

        def _rope_cache(seq_len, head_dim, theta):
            inv_freq = 1.0 / theta ** (jnp.arange(0, head_dim, 2, dtype=jnp.float32) / head_dim)
            pos = jnp.arange(seq_len, dtype=jnp.float32)
            freqs = pos[:, None] * inv_freq[None, :]
            emb = jnp.concatenate([freqs, freqs], axis=-1)
            return (jnp.cos(emb), jnp.sin(emb))

        def _rotate_half(x):
            x1, x2 = jnp.split(x, 2, axis=-1)
            return jnp.concatenate([-x2, x1], axis=-1)
        b, s, _ = hidden_states.shape
        q = jnp.einsum('bsh,oh->bso', hidden_states, Wq).reshape(b, s, H, D).transpose(0, 2, 1, 3)
        k = jnp.einsum('bsh,oh->bso', hidden_states, Wk).reshape(b, s, KV, D).transpose(0, 2, 1, 3)
        v = jnp.einsum('bsh,oh->bso', hidden_states, Wv).reshape(b, s, KV, D).transpose(0, 2, 1, 3)
        cos, sin = _rope_cache(s, D, THETA)
        cos = cos[None, None]
        sin = sin[None, None]
        q = q * cos + _rotate_half(q) * sin
        k = k * cos + _rotate_half(k) * sin
        q = _layernorm_unit(q) * SCALAR
        k = _layernorm_unit(k)
        v = _layernorm_unit(v)
        rep = H // KV
        k = jnp.repeat(k, rep, axis=1)
        v = jnp.repeat(v, rep, axis=1)
        scores = jnp.einsum('bhqd,bhkd->bhqk', q, k) / jnp.sqrt(jnp.float32(D))
        i = jnp.arange(s)[:, None]
        j = jnp.arange(s)[None, :]
        allowed = (j <= i) & (j > i - SW)
        mask = jnp.where(allowed, 0.0, -jnp.inf).astype(scores.dtype)
        scores = scores + mask
        scores = jnp.tanh(scores / SOFTCAP) * SOFTCAP
        probs = jax.nn.softmax(scores.astype(jnp.float32), axis=-1).astype(v.dtype)
        out = jnp.einsum('bhqk,bhkd->bhqd', probs, v)
        out = out.transpose(0, 2, 1, 3).reshape(b, s, H * D)
        return jnp.einsum('bso,ho->bsh', out, Wo)

    def _L0_ffn_ref(x, gate_w, expert_bias, w1, w2, w3, sw1, sw2, sw3):
        import jax, jax.numpy as jnp
        import numpy as np
        DIM = 256
        INTER = 176
        E = 16
        TOPK = 4
        G = 4
        TOPK_G = 2
        N_SHARED = 2
        ROUTE_SCALE = 1.0
        INIT_STD = 0.02
        B, S = (1, 256)
        b, s, d = x.shape
        T = b * s
        xf = x.reshape(T, d)
        scores = jax.nn.sigmoid(xf @ gate_w.T)
        original_scores = scores
        scores = scores + expert_bias
        sg = scores.reshape(T, G, E // G)
        group_scores = sg.max(axis=-1)
        _, gidx = jax.lax.top_k(group_scores, TOPK_G)
        gmask = jnp.zeros((T, G), bool).at[jnp.arange(T)[:, None], gidx].set(True)
        masked = jnp.where(gmask[:, :, None], sg, -jnp.inf).reshape(T, E)
        _, idx = jax.lax.top_k(masked, TOPK)
        w = jnp.take_along_axis(original_scores, idx, axis=1)
        w = w / jnp.sum(w, axis=-1, keepdims=True)
        w = w * ROUTE_SCALE
        cw = jnp.zeros((T, E), x.dtype).at[jnp.arange(T)[:, None], idx].add(w)
        h = jax.nn.silu(jnp.einsum('td,edh->teh', xf, w1)) * jnp.einsum('td,edh->teh', xf, w3)
        y = jnp.einsum('teh,ehd,te->td', h, w2, cw)
        z = jax.nn.silu(xf @ sw1) * (xf @ sw3) @ sw2
        return (y + z).reshape(b, s, d)
    x = L0_attn_hidden_states
    mod = (_silu(L0_c) @ L0_wmod).reshape(L0_c.shape[0], 6, 1, -1)
    sa, ca, ga, sb, cb, gb = (mod[:, 0], mod[:, 1], mod[:, 2], mod[:, 3], mod[:, 4], mod[:, 5])
    ga = (2 * (ga >= 0) - 1) * jnp.maximum(jnp.abs(ga), 0.25)
    gb = (2 * (gb >= 0) - 1) * jnp.maximum(jnp.abs(gb), 0.25)
    h = _layernorm(x, axis=-1) * (1 + ca) + sa
    x = x + ga * _L0_attn_ref(h, L0_attn_Wq, L0_attn_Wk, L0_attn_Wv, L0_attn_Wo)
    h = _layernorm(x, axis=-1) * (1 + cb) + sb
    x = x + gb * _L0_ffn_ref(h, L0_ffn_gate_w, L0_ffn_expert_bias, L0_ffn_w1, L0_ffn_w2, L0_ffn_w3, L0_ffn_sw1, L0_ffn_sw2, L0_ffn_sw3)
    return x

_drawn_inputs = setup_inputs


def setup_inputs(seed=0):
    import zlib

    import numpy as np

    out = dict(_drawn_inputs(seed))
    spreads = {'L0_ffn_expert_bias': (0.0, 0.8)}
    factors = {'L0_attn_Wq': 3.422,
     'L0_attn_Wk': 3.396,
     'L0_attn_Wv': 2.682,
     'L0_attn_Wo': 2.671,
     'L0_ffn_gate_w': 8.0,
     'L0_ffn_w1': 8.0,
     'L0_ffn_w2': 8.0,
     'L0_ffn_w3': 8.0,
     'L0_ffn_sw1': 8.0,
     'L0_ffn_sw2': 8.0,
     'L0_ffn_sw3': 8.0}
    for name, (base, spread) in spreads.items():
        noise = np.random.default_rng([zlib.crc32(name.encode()), seed]).standard_normal(out[name].shape)
        drawn = base * np.exp(spread * noise) if base else spread * noise
        out[name] = jnp.asarray(drawn.astype(out[name].dtype))
    for name, factor in factors.items():
        out[name] = (out[name] * factor).astype(out[name].dtype)
    return out
```

```python
from contextlib import ExitStack

import numpy as np

import concourse.bass as bass
from concourse import mybir

ALU = mybir.AluOpType
ACT = mybir.ActivationFunctionType
AX = mybir.AxisListType
F32 = mybir.dt.float32
F32R = mybir.dt.float32r
BF16 = mybir.dt.bfloat16
U32 = mybir.dt.uint32

P = 128
B, S, HID = 8, 256, 256
QT = S // P
NT = B * QT
KC = HID // P
H, KV, D = 8, 2, 32
REP = H // KV
QKV = (H + 2 * KV) * D
NG = H + 2 * KV
WINDOW = 64
SOFTCAP = 30.0
Q_SCALE = 256.0
THETA = 1000000.0
SCORE_TO_TANH = Q_SCALE / float(np.sqrt(np.float32(D))) / SOFTCAP
MASKED_P = float(np.exp(np.float32(-SOFTCAP)))
LN_EPS, QK_EPS = 1e-5, 1e-6

E, INTER, TOPK, G, TOPK_G = 16, 176, 4, 4, 2
EG = E // G
SHARED = 2
NE = E + SHARED
HA = 112
HB = INTER - HA
HW = INTER + HB
FAR = 1e30

K1, K0, SC = 128, 192, 320
PC = 384


def constants():
    inv = (1.0 / np.float32(THETA) ** (np.arange(0, D, 2, dtype=np.float32) / np.float32(D))).astype(np.float32)
    freqs = np.arange(S, dtype=np.float32)[:, None] * inv[None, :]
    cos, sin = np.cos(freqs).astype(np.float32), np.sin(freqs).astype(np.float32)
    rope = np.stack([np.concatenate([cos, cos], 1), np.concatenate([-sin, sin], 1)], 1)
    rope = rope.reshape(QT, P, 2, D).transpose(1, 2, 0, 3)
    lower = (np.arange(G)[None, :] < np.arange(G)[:, None]).astype(np.float32)
    key, col = np.arange(P)[:, None], np.arange(SC)[None, :]
    key, query = np.where(col < K1, key + P, key), np.where(col < K1, col + P, col - K1)
    allowed = (key <= query) & (key > query - WINDOW)
    return {
        "mask": np.where(allowed, 0.0, -1e5).astype(np.float32),
        "rope": np.ascontiguousarray(rope),
        "ident": np.eye(P, dtype=np.float32),
        "lower": np.ascontiguousarray(np.broadcast_to(lower.reshape(1, G * G), (P, G * G))),
        "iota": np.ascontiguousarray(np.broadcast_to(np.arange(E, dtype=np.float32), (P, E))),
    }


def build(nc, a, out):
    with ExitStack() as whole:
        def sb(name, shape, dt=F32, ctx=whole):
            return ctx.enter_context(nc.sbuf_tensor(name, shape, dt))

        mod_rows = nc.dram_tensor("mod_rows", [B, 4, HID], F32, kind="Internal").ap()

        x1 = sb("x1", [P, NT, HID])
        h2 = sb("h2", [P, NT, HID])
        gate_t = sb("gate_t", [P, NT, E])
        cw = sb("cw", [P, NT, NE])
        ident = sb("ident", [P, P])
        attention(nc, a, mod_rows, x1, h2, gate_t, ident)
        routing(nc, a, gate_t, cw)
        ffn(nc, a, out, mod_rows, x1, h2, cw, ident)


def named(semaphores):
    return type("Semaphores", (), semaphores)


def after(eng, sem, count):
    if not (isinstance(count, int) and count <= 0):
        eng.wait_ge(sem, count)


def attention(nc, a, mod_rows, x1, h2, gate_t, ident):
    with ExitStack() as ctx:
        def sb(name, shape, dt=F32):
            return ctx.enter_context(nc.sbuf_tensor(name, shape, dt))

        def sem(name):
            return ctx.enter_context(nc.semaphore(name))

        wqkv = sb("wqkv", [P, KC, QKV])
        wqkvh = sb("wqkvh", [P, KC, QKV], F32R)
        wqkvl = sb("wqkvl", [P, KC, QKV], F32R)
        wo = sb("wo", [P, KC, HID])
        woh = sb("woh", [P, KC, HID], F32R)
        wol = sb("wol", [P, KC, HID], F32R)
        wgate = sb("wgate", [P, KC, E])
        rope = sb("rope", [P, 2, QT, D])
        ct = sb("ct", [P, KC, B])
        ct_tanh = sb("ct_tanh", [P, KC, B])
        ct_silu = sb("ct_silu", [P, KC, B])
        wmod = sb("wmod", [P, KC, 6 * HID])
        mod_cols = sb("mod_cols", [P, 4, B])
        rows = sb("rows", [B, 4, HID])
        rows_neg = sb("rows_neg", [B, 2, HID])
        rows_sign = sb("rows_sign", [B, 2, HID])
        mask_f = sb("mask_f", [P, SC])
        mask = sb("mask", [P, SC], BF16)
        ident_b = sb("ident_b", [P, P], BF16)
        masked = sb("masked", [P, P])
        minus_half = sb("minus_half", [P, 2 * NG])
        mod = sb("mod", [P, 2, 3, HID])
        stats = sb("stats", [P, QT, 6])
        mv = sb("mv", [P, QT, 2])
        veps = sb("veps", [P, QT])
        veps2 = sb("veps2", [P, QT])
        meansq = sb("meansq", [P, QT * NG])
        rstd = sb("rstd", [P, QT])
        xhat = sb("xhat", [P, QT, HID])
        ht = sb("ht", [P, KC, S])
        hth = sb("hth", [P, KC, S], F32R)
        htl = sb("htl", [P, KC, S], F32R)
        qkv = sb("qkv", [P, QT, QKV])
        rcos = sb("rcos", [P, QT, (H + KV) * D])
        rsin = sb("rsin", [P, QT, (H + KV) * D])
        sums = sb("sums", [P, QT * NG])
        squares = sb("squares", [P, QT, QKV])
        sumsq = sb("sumsq", [P, QT * NG])
        rn = sb("rn", [P, QT * NG])
        qn = sb("qn", [P, QT, H * D])
        kn = sb("kn", [P, QT, KV, REP, D])
        v = sb("v", [P, 2, QT, KV, D + 1])
        qt = sb("qt", [P, 2, KV, S])
        kt = sb("kt", [P, 2, KV, S])
        capped = sb("capped", [P, REP, SC])
        probs = sb("probs", [P, 2, REP, PC])
        rden = sb("rden", [P, QT, REP])
        attn = sb("attn", [P, QT, H * D])
        oth = sb("oth", [P, KC, S], F32R)
        otl = sb("otl", [P, KC, S], F32R)
        gated = sb("gated", [P, QT, HID])
        stats2 = sb("stats2", [P, QT, 6])
        mv2 = sb("mv2", [P, QT, 2])
        rstd2 = sb("rstd2", [P, QT])
        xhat2 = sb("xhat2", [P, QT, HID])
        scaled2 = sb("scaled2", [P, QT, HID])
        tick = sb("tick", [P, 1])
        h2b = sb("h2b", [P, QT, HID])
        h2t = sb("h2t", [P, KC, S])

        sc_ps = ctx.enter_context(nc.psum_tensor("sc_ps", [P, REP, 512], F32))
        tp = ctx.enter_context(nc.psum_tensor("tp", [P, KC, S], F32))
        qkv_ps = ctx.enter_context(nc.psum_tensor("qkv_ps", [P, QT, 512], F32))
        pv = ctx.enter_context(nc.psum_tensor("pv", [P, 512], F32))

        s = named({n: sem(n) for n in (
            "c_in w_in wmod_in wo_in ct_tanh_done ct_silu_done cols_mm rows_mm cols_done rows_copied rows_neg_done "
            "rows_sign_done rows_sign2 rows_done rows_stored consts_set pool_consts wqkvh_done wqkvl_done woh_done wol_done "
            "stats_done mv_done var_eps rstd_done xhat_done xhat_t ht_done hth_done htl_done qkv_mm qkv_done rcos_done rsin_done "
            "rot_done sums_done centered squared sumsq_done rn_eps rn_done q_done k_done v_done q_t qt_done k_t kt_done scores_mm "
            "tanh_done mask_set probs_done pv_mm rden_done attn_done attn_t oth_done otl_done wo_mm gated_done x1_done "
            "stats2_done mv2_done var2_eps rstd2_done xhat2_done scaled2_done h2_done h2_t h2t_done h2_kept logits_mm gate_done").split()})

        x_in = [sem(f"x_in{b}") for b in range(B // 2)]
        mod_in = [sem(f"mod_in{p}") for p in range(2)]

        block = ctx.enter_context(nc.Block())

        def batches(eng, step):
            step(-1, 1, lead=True)
            step(0, 0, lead=True, here=True)
            step(1, 1, lead=True, here=True, lag=True)
            with eng.Fori(1, B // 2 - 1) as i:
                for p in range(2):
                    step(i * 2 + p, p, lead=True, here=True, lag=True)
            step(B - 2, 0, lead=True, here=True, lag=True)
            step(B - 1, 1, here=True, lag=True)
            step(B, 0, lag=True)

        @block.sync
        def _(sp):
            sp.dma_start(ct[:], a["ct"]).then_inc(s.c_in, 16)
            sp.dma_start(wmod[:], a["wmod"]).then_inc(s.wmod_in, 16)

            def load_x(b):
                src = a["x"][2 * b:2 * b + 2].rearrange("b (t p) h -> p (b t) h", p=P)
                sp.dma_start(x1[:, 2 * b * QT:(2 * b + 2) * QT], src).then_inc(x_in[b], 16)

            def load_mod(b, p):
                if not (isinstance(b, int) and b < 2):
                    sp.wait_ge(s.h2_done, b - 1)
                src = mod_rows[bass.ds(b, 1), 0:3].rearrange("o r h -> o (r h)").to_broadcast([P, 3 * HID])
                sp.dma_start(mod[:, p].rearrange("p r h -> p (r h)"), src).then_inc(mod_in[p], 16)

            load_x(0)
            sp.dma_start(ident[:], a["ident"]).then_inc(s.w_in, 16)
            sp.dma_start(wqkv[:], a["wqkv"]).then_inc(s.w_in, 16)
            sp.dma_start(rope[:], a["rope"]).then_inc(s.w_in, 16)
            sp.dma_start(mask_f[:], a["mask"]).then_inc(s.w_in, 16)
            sp.dma_start(wo[:], a["wo"]).then_inc(s.wo_in, 16)
            sp.dma_start(wgate[:], a["wgate"]).then_inc(s.wo_in, 16)
            for b in range(1, B // 2):
                load_x(b)
            sp.wait_ge(s.rows_done, 2)
            sp.dma_start(mod_rows.rearrange("b r h -> b (r h)"), rows[:].rearrange("b r h -> b (r h)")).then_inc(s.rows_stored, 16)
            sp.wait_ge(s.rows_stored, 16)
            load_mod(0, 0)
            load_mod(1, 1)
            with sp.Fori(1, B // 2) as i:
                for p in range(2):
                    load_mod(i * 2 + p, p)

        @block.gpsimd
        def _(pool):
            pool.memset(minus_half[:], -0.5).then_inc(s.pool_consts, 1)
            pool.memset(masked[:], MASKED_P).then_inc(s.pool_consts, 1)
            pool.memset(v[:, :, :, :, D:D + 1], 1.0).then_inc(s.pool_consts, 1)
            pool.memset(probs[:, :, :, SC:PC], MASKED_P).then_inc(s.pool_consts, 1)

            def first_rstd(b):
                pool.wait_ge(s.var_eps, b + 1)
                pool.tensor_tensor(rstd[:], veps[:], minus_half[:, 0:QT], ALU.pow).then_inc(s.rstd_done, 1)

            def rotate_sin(b):
                pool.wait_ge(s.qkv_done, b + 1)
                after(pool, s.rot_done, b)
                half = D // 2
                for t in range(QT):
                    src = qkv[:, t, 0:(H + KV) * D].rearrange("p (g d) -> p g d", d=D)
                    dst = rsin[:, t].rearrange("p (g d) -> p g d", d=D)
                    for lo, frm in ((0, half), (half, 0)):
                        tab = rope[:, 1, t, lo:lo + half].unsqueeze(1).to_broadcast([P, H + KV, half])
                        pool.tensor_tensor(dst[:, :, lo:lo + half], src[:, :, frm:frm + half], tab, ALU.mult).then_inc(s.rsin_done, 1)

            def group_rstd(b):
                pool.wait_ge(s.rn_eps, b + 1)
                pool.tensor_tensor(rn[:], meansq[:], minus_half[:], ALU.pow).then_inc(s.rn_done, 1)

            def normed_kv(b, p):
                after(pool, s.k_t, b)
                after(pool, s.pv_mm, 2 * b - 2)
                pool.wait_ge(s.rn_done, b + 1)
                for t in range(QT):
                    pool.tensor_tensor(
                        v[:, p, t, :, 0:D], qkv[:, t, (H + KV) * D:].rearrange("p (g d) -> p g d", d=D),
                        rn[:, t * NG + H + KV:(t + 1) * NG].unsqueeze(2).to_broadcast([P, KV, D]), ALU.mult).then_inc(s.v_done, 1)
                for t in range(QT):
                    for c in range(KV):
                        pool.tensor_scalar(kn[:, t, c], qkv[:, t, (H + c) * D:(H + c + 1) * D].unsqueeze(1).to_broadcast([P, REP, D]),
                                           rn[:, t * NG + H + c:t * NG + H + c + 1], None, ALU.mult).then_inc(s.k_done, 1)

            def modulate(b, p):
                pool.wait_ge(s.xhat2_done, (b + 1) * QT)
                pool.tensor_tensor(scaled2[:], xhat2[:], mod[:, p, 2:3].to_broadcast([P, QT, HID]), ALU.mult).then_inc(s.scaled2_done, 1)
                pool.wait_ge(s.scaled2_done, b + 1)
                after(pool, s.h2_t, b)
                after(pool, s.h2_kept, b)
                pool.tensor_tensor(h2b[:], scaled2[:], mod[:, p, 1:2].to_broadcast([P, QT, HID]), ALU.add).then_inc(s.h2_done, 1)

            def step(b, p, lead=False, here=False, lag=False):
                if lead and isinstance(b, int) and b < 0:
                    pool.wait_ge(s.pool_consts, 4)
                    first_rstd(0)
                    pool.wait_ge(s.w_in, 64)
                if lead:
                    rotate_sin(b + 1)
                    group_rstd(b + 1)
                if lag:
                    pool.wait_ge(s.var2_eps, b)
                    pool.tensor_tensor(rstd2[:], veps2[:], minus_half[:, 0:QT], ALU.pow).then_inc(s.rstd2_done, 1)
                if lead:
                    normed_kv(b + 1, 1 - p)
                if lag:
                    modulate(b - 1, 1 - p)
                if lead and not (isinstance(b, int) and b == B - 2):
                    first_rstd(b + 2)

            batches(pool, step)

        @block.scalar
        def _(act):
            act.wait_ge(s.c_in, 16)
            act.activation(ct_tanh[:], ct[:], ACT.Tanh, scale=0.5).then_inc(s.ct_tanh_done, 1)
            act.wait_ge(s.rows_mm, 1)
            act.activation(rows[:].rearrange("b r h -> b (r h)")[:, 0:512], sc_ps[0:B, 0, :], ACT.Copy).then_inc(s.rows_copied, 1)
            act.activation(rows[:].rearrange("b r h -> b (r h)")[:, 512:1024], sc_ps[0:B, 1, :], ACT.Copy).then_inc(s.rows_copied, 1)
            act.wait_ge(s.w_in, 64)
            act.activation(wqkvh[:], wqkv[:], ACT.Copy).then_inc(s.wqkvh_done, 1)
            act.activation(mask[:], mask_f[:], ACT.Copy).then_inc(s.mask_set, 1)
            act.activation(ident_b[:], ident[:], ACT.Copy).then_inc(s.mask_set, 1)
            act.wait_ge(s.wo_in, 32)
            act.activation(woh[:], wo[:], ACT.Copy).then_inc(s.woh_done, 1)
            act.wait_ge(s.cols_done, 2)

            def modulated(b):
                act.wait_ge(s.xhat_t, b + 1)
                after(act, s.htl_done, b)
                after(act, s.qkv_mm, b)
                for c in range(KC):
                    scale, shift = (mod_cols[:, 2 * r + c, bass.ds(b, 1)] for r in (1, 0))
                    act.activation(ht[:, c], tp[:, c], ACT.Identity, scale=scale, bias=shift).then_inc(s.ht_done, 1)
                    act.activation(hth[:, c], tp[:, c], ACT.Identity, scale=scale, bias=shift).then_inc(s.hth_done, 1)

            def copy_qkv(b):
                act.wait_ge(s.qkv_mm, b + 1)
                after(act, s.q_done, b)
                after(act, s.k_done, b * QT * KV)
                after(act, s.v_done, b * QT)
                act.activation(qkv[:], qkv_ps[:, :, 0:QKV], ACT.Copy).then_inc(s.qkv_done, 1)

            def square(b):
                act.wait_ge(s.centered, b + 1)
                after(act, s.sumsq_done, b)
                act.activation(squares[:], qkv[:], ACT.Square).then_inc(s.squared, 1)

            def copy_qkt(b, p):
                after(act, s.scores_mm, 2 * b - 2)
                act.wait_ge(s.q_t, b + 1)
                act.activation(qt[:, p], tp[:], ACT.Copy).then_inc(s.qt_done, 1)
                act.wait_ge(s.k_t, b + 1)
                act.activation(kt[:, p].rearrange("p g q -> p (g q)"), qkv_ps[:, 0, :], ACT.Copy).then_inc(s.kt_done, 1)

            def cap(b, g):
                n = b * 2 + g
                act.wait_ge(s.scores_mm, n + 1)
                after(act, s.probs_done, n)
                act.activation(capped[:], sc_ps[:, :, 0:SC], ACT.Tanh, scale=SCORE_TO_TANH).then_inc(s.tanh_done, 1)

            def exps(b, g):
                n = b * 2 + g
                act.wait_ge(s.tanh_done, n + 1)
                act.wait_ge(s.pool_consts, 4)
                after(act, s.pv_mm, 2 * b)
                act.activation(probs[:, g, :, 0:SC], capped[:], ACT.Exp, scale=SOFTCAP).then_inc(s.probs_done, 1)

            def step(b, p, lead=False, here=False, lag=False):
                if lead:
                    modulated(b + 1)
                if here:
                    cap(b, 0)
                if lag:
                    act.wait_ge(s.attn_t, b)
                    after(act, s.wo_mm, b - 1)
                    act.activation(oth[:], tp[:], ACT.Copy).then_inc(s.oth_done, 1)
                if lead:
                    copy_qkv(b + 1)
                if here:
                    exps(b, 0)
                    cap(b, 1)
                if lead:
                    square(b + 1)
                if here:
                    exps(b, 1)
                if lag:
                    act.wait_ge(s.h2_done, b)
                    act.activation(h2[:, bass.ds(b * 2 - 2, QT)], h2b[:], ACT.Copy).then_inc(s.h2_kept, 1)
                    act.wait_ge(s.h2_t, b)
                    after(act, s.logits_mm, b - 1)
                    act.activation(h2t[:], tp[:], ACT.Copy).then_inc(s.h2t_done, 1)
                    act.wait_ge(s.logits_mm, b)
                    act.activation(gate_t[:, bass.ds(b * 2 - 2, QT)], pv[:, 0:QT * E].rearrange("p (t e) -> p t e", e=E),
                                   ACT.Tanh, scale=0.5).then_inc(s.gate_done, 1)
                if lead:
                    copy_qkt(b + 1, 1 - p)

            batches(act, step)

        @block.vector
        def _(dve):
            def gate_dve():
                dve.memset(tick[:], 0.0)

            dve.wait_ge(s.ct_tanh_done, 1)
            dve.tensor_scalar(ct_tanh[:], ct_tanh[:], 0.5, 0.5, ALU.mult, ALU.add).then_inc(s.consts_set, 1)
            dve.wait_ge(s.consts_set, 1)
            dve.tensor_tensor(ct_silu[:], ct_tanh[:], ct[:], ALU.mult).then_inc(s.ct_silu_done, 1)
            dve.wait_ge(s.cols_mm, 1)
            cols = pv[:, 0:4 * B].rearrange("p (m b) -> p m b", b=B)
            dve.tensor_copy(mod_cols[:, 0:2], cols[:, 0:2]).then_inc(s.cols_done, 1)
            dve.tensor_scalar(mod_cols[:, 2:4], cols[:, 2:4], 1.0, None, ALU.add).then_inc(s.cols_done, 1)
            dve.wait_ge(s.rows_copied, 2)
            dve.tensor_scalar(rows[:, 2], rows[:, 2], 1.0, None, ALU.add).then_inc(s.rows_done, 1)
            gates = rows[:, 0:4:3]
            dve.tensor_scalar(rows_neg[:], gates, -1.0, None, ALU.mult).then_inc(s.rows_neg_done, 1)
            dve.tensor_scalar(rows_sign[:], gates, 0.0, None, ALU.is_ge).then_inc(s.rows_sign_done, 1)
            dve.wait_ge(s.rows_neg_done, 1)
            dve.tensor_tensor(rows_neg[:], rows_neg[:], gates, ALU.max).then_inc(s.rows_neg_done, 1)
            dve.wait_ge(s.rows_sign_done, 1)
            dve.tensor_scalar(rows_sign[:], rows_sign[:], 2.0, -1.0, ALU.mult, ALU.add).then_inc(s.rows_sign_done, 1)
            dve.wait_ge(s.rows_neg_done, 2)
            dve.wait_ge(s.rows_sign_done, 2)
            dve.scalar_tensor_tensor(out=gates, in0=rows_neg[:], scalar=0.25, in1=rows_sign[:], op0=ALU.max, op1=ALU.mult).then_inc(s.rows_done, 1)
            dve.wait_ge(s.wqkvh_done, 1)
            dve.tensor_tensor(wqkvl[:], wqkv[:], wqkvh[:].bitcast(F32), ALU.subtract).then_inc(s.wqkvl_done, 1)
            dve.wait_ge(s.woh_done, 1)
            dve.tensor_tensor(wol[:], wo[:], woh[:].bitcast(F32), ALU.subtract).then_inc(s.wol_done, 1)

            def layernorm1(b):
                if isinstance(b, int):
                    if b % 2 == 0:
                        dve.wait_ge(x_in[b // 2], 16)
                        gate_dve()
                else:
                    for n in range(1, B // 2):
                        dve.wait_ge(x_in[n], 16)
                    gate_dve()
                for t in range(QT):
                    dve.bn_stats(stats[:, t], x1[:, bass.ds(b * 2 + t, 1)]).then_inc(s.stats_done, 1)
                dve.wait_ge(s.stats_done, 2 * b + 2)
                gate_dve()
                for t in range(QT):
                    dve.bn_aggr(mv[:, t], stats[:, t]).then_inc(s.mv_done, 1)
                dve.wait_ge(s.mv_done, 2 * b + 2)
                dve.tensor_scalar(veps[:], mv[:, :, 1], LN_EPS, None, ALU.add).then_inc(s.var_eps, 1)
                after(dve, s.xhat_t, b)
                dve.wait_ge(s.rstd_done, b + 1)
                for t in range(QT):
                    dve.tensor_scalar(xhat[:, t], x1[:, bass.ds(b * 2 + t, 1)].rearrange("p o h -> p (o h)"), mv[:, t, 0:1], rstd[:, t:t + 1],
                                      ALU.subtract, ALU.mult).then_inc(s.xhat_done, 1)

            def rotate_cos(b):
                dve.wait_ge(s.qkv_done, b + 1)
                for t in range(QT):
                    tab = rope[:, 0, t].unsqueeze(1).to_broadcast([P, H + KV, D])
                    dve.tensor_tensor(rcos[:, t].rearrange("p (g d) -> p g d", d=D), qkv[:, t, 0:(H + KV) * D].rearrange("p (g d) -> p g d", d=D),
                                      tab, ALU.mult).then_inc(s.rcos_done, 1)

            groups = qkv[:].rearrange("p t (g d) -> p (t g) d", d=D)

            def centre(b):
                dve.wait_ge(s.rcos_done, (b + 1) * QT)
                dve.wait_ge(s.rsin_done, (b + 1) * 2 * QT)
                dve.tensor_tensor(qkv[:, :, 0:(H + KV) * D], rcos[:], rsin[:], ALU.add).then_inc(s.rot_done, 1)
                dve.wait_ge(s.rot_done, b + 1)
                dve.tensor_reduce(sums[:], groups, AX.X, ALU.add).then_inc(s.sums_done, 1)
                dve.wait_ge(s.sums_done, b + 1)
                dve.scalar_tensor_tensor(out=groups, in0=sums[:].unsqueeze(2).to_broadcast([P, QT * NG, D]), scalar=-1.0 / D, in1=groups,
                                         op0=ALU.mult, op1=ALU.add).then_inc(s.centered, 1)

            def mean_square(b):
                dve.wait_ge(s.squared, b + 1)
                dve.tensor_reduce(sumsq[:], squares[:].rearrange("p t (g d) -> p (t g) d", d=D), AX.X, ALU.add).then_inc(s.sumsq_done, 1)
                dve.wait_ge(s.sumsq_done, b + 1)
                dve.tensor_scalar(meansq[:], sumsq[:], 1.0 / D, QK_EPS, ALU.mult, ALU.add).then_inc(s.rn_eps, 1)

            def normed_q(b):
                dve.wait_ge(s.rn_done, b + 1)
                after(dve, s.q_t, b)
                dve.tensor_tensor(qn[:].rearrange("p t (g d) -> p t g d", d=D), qkv[:, :, 0:H * D].rearrange("p t (g d) -> p t g d", d=D),
                                  rn[:].rearrange("p (t g) -> p t g", g=NG)[:, :, 0:H].unsqueeze(3).to_broadcast([P, QT, H, D]),
                                  ALU.mult).then_inc(s.q_done, 1)

            def normalise(b, g):
                n = b * 2 + g
                dve.wait_ge(s.pv_mm, n + 1)
                o = pv[:, 0:QT * REP * (D + 1)].rearrange("p (t h d) -> p t h d", t=QT, h=REP)
                after(dve, s.attn_done, n)
                dve.reciprocal(rden[:].unsqueeze(3), o[:, :, :, D:D + 1]).then_inc(s.rden_done, 1)
                if g == 0:
                    after(dve, s.attn_t, b)
                dve.wait_ge(s.rden_done, n + 1)
                dve.tensor_tensor(attn[:, :, g * REP * D:(g + 1) * REP * D].rearrange("p t (h d) -> p t h d", d=D), o[:, :, :, 0:D],
                                  rden[:].unsqueeze(3).to_broadcast([P, QT, REP, D]), ALU.mult).then_inc(s.attn_done, 1)

            def residual(b, p):
                dve.wait_ge(s.wo_mm, b + 1)
                dve.wait_ge(mod_in[p], 8 * (b - p) + 16)
                dve.tensor_tensor(gated[:], qkv_ps[:, 1].rearrange("p (t h) -> p t h", t=QT), mod[:, p, 0:1].to_broadcast([P, QT, HID]), ALU.mult)\
                    .then_inc(s.gated_done, 1)
                dve.wait_ge(s.gated_done, b + 1)
                x1_b = x1[:, bass.ds(b * 2, QT)]
                dve.tensor_tensor(x1_b, gated[:], x1_b, ALU.add).then_inc(s.x1_done, 1)

            def layernorm2(b):
                dve.wait_ge(s.x1_done, b + 1)
                gate_dve()
                for t in range(QT):
                    dve.bn_stats(stats2[:, t], x1[:, bass.ds(b * 2 + t, 1)]).then_inc(s.stats2_done, 1)
                dve.wait_ge(s.stats2_done, 2 * b + 2)
                gate_dve()
                for t in range(QT):
                    dve.bn_aggr(mv2[:, t], stats2[:, t]).then_inc(s.mv2_done, 1)
                dve.wait_ge(s.mv2_done, 2 * b + 2)
                dve.tensor_scalar(veps2[:], mv2[:, :, 1], LN_EPS, None, ALU.add).then_inc(s.var2_eps, 1)

            def normed2(b):
                after(dve, s.scaled2_done, b)
                dve.wait_ge(s.rstd2_done, b + 1)
                for t in range(QT):
                    dve.tensor_scalar(xhat2[:, t], x1[:, bass.ds(b * 2 + t, 1)].rearrange("p o h -> p (o h)"), mv2[:, t, 0:1], rstd2[:, t:t + 1],
                                      ALU.subtract, ALU.mult).then_inc(s.xhat2_done, 1)

            def step(b, p, lead=False, here=False, lag=False):
                if lead:
                    if isinstance(b, int) and b < 0:
                        layernorm1(0)
                    dve.wait_ge(s.ht_done, (b + 2) * KC)
                    dve.wait_ge(s.hth_done, (b + 2) * KC)
                    after(dve, s.qkv_mm, b + 1)
                    dve.tensor_tensor(htl[:], ht[:], hth[:].bitcast(F32), ALU.subtract).then_inc(s.htl_done, 1)
                if lag:
                    dve.wait_ge(s.oth_done, b)
                    after(dve, s.wo_mm, b - 1)
                    dve.tensor_tensor(otl[:], tp[:], oth[:].bitcast(F32), ALU.subtract).then_inc(s.otl_done, 1)
                if lead:
                    rotate_cos(b + 1)
                if here:
                    normalise(b, 0)
                if lead:
                    centre(b + 1)
                if lag:
                    residual(b - 1, 1 - p)
                    layernorm2(b - 1)
                if lead:
                    mean_square(b + 1)
                if lag:
                    normed2(b - 1)
                if lead:
                    normed_q(b + 1)
                if here:
                    normalise(b, 1)
                if lead and not (isinstance(b, int) and b == B - 2):
                    layernorm1(b + 2)

            batches(dve, step)

        @block.tensor
        def _(pe):
            pe.wait_ge(s.ct_silu_done, 1)
            pe.wait_ge(s.wmod_in, 16)
            for m in range(4):
                for k in range(KC):
                    mm = pe.matmul(pv[:, m * B:(m + 1) * B], wmod[:, k, m * P:(m + 1) * P], ct_silu[:, k], start=(k == 0), stop=(k == KC - 1))
            mm.then_inc(s.cols_mm, 1)
            for m in range(2):
                for k in range(KC):
                    mm = pe.matmul(sc_ps[0:B, m], ct_silu[:, k], wmod[:, k, 512 + m * 512:1024 + m * 512], start=(k == 0), stop=(k == KC - 1))
            mm.then_inc(s.rows_mm, 1)

            def split3(out_ap, xh, xl, wh, wl):
                n = len(xh)
                for k in range(n):
                    pe.matmul(out_ap, xh[k], wh[k], start=(k == 0), stop=False)
                    pe.matmul(out_ap, xh[k], wl[k], start=False, stop=False)
                    mm = pe.matmul(out_ap, xl[k], wh[k], start=False, stop=(k == n - 1))
                return mm

            def turn_xhat(b):
                pe.wait_ge(s.xhat_done, (b + 1) * QT)
                if isinstance(b, int) and b == 0:
                    pe.wait_ge(s.w_in, 64)
                else:
                    pe.wait_ge(s.qt_done, b)
                for t in range(QT):
                    for c in range(KC):
                        mm = pe.transpose(tp[:, c, t * P:(t + 1) * P], xhat[:, t, c * P:(c + 1) * P], ident[:])
                mm.then_inc(s.xhat_t, 1)

            def project(b):
                pe.wait_ge(s.htl_done, b + 1)
                pe.wait_ge(s.hth_done, (b + 1) * KC)
                if isinstance(b, int) and b == 0:
                    pe.wait_ge(s.wqkvl_done, 1)
                else:
                    pe.wait_ge(s.kt_done, b)
                    after(pe, s.gated_done, b - 2)
                for t in range(QT):
                    mm = split3(qkv_ps[:, t, 0:QKV], [hth[:, c, t * P:(t + 1) * P] for c in range(KC)], [htl[:, c, t * P:(t + 1) * P] for c in range(KC)],
                                [wqkvh[:, c] for c in range(KC)], [wqkvl[:, c] for c in range(KC)])
                mm.then_inc(s.qkv_mm, 1)

            def turn_qk(b, lag):
                pe.wait_ge(s.q_done, b + 1)
                pe.wait_ge(s.ht_done, (b + 1) * KC)
                pe.wait_ge(s.hth_done, (b + 1) * KC)
                if lag:
                    pe.wait_ge(s.h2t_done, b - 1)
                for t in range(QT):
                    for c in range(KV):
                        mm = pe.transpose(tp[:, c, t * P:(t + 1) * P], qn[:, t, c * P:(c + 1) * P], ident[:])
                mm.then_inc(s.q_t, 1)
                pe.wait_ge(s.k_done, (b + 1) * QT * KV)
                pe.wait_ge(s.qkv_done, b + 1)
                for t in range(QT):
                    for c in range(KV):
                        mm = pe.transpose(qkv_ps[:, 0, c * S + t * P:c * S + (t + 1) * P], kn[:, t, c].rearrange("p r d -> p (r d)"), ident[:])
                mm.then_inc(s.k_t, 1)

            def scores(b, p, g):
                n = b * 2 + g
                if g == 0:
                    pe.wait_ge(s.qt_done, b + 1)
                    pe.wait_ge(s.kt_done, b + 1)
                if isinstance(b, int) and n == 0:
                    pe.wait_ge(s.rows_copied, 2)
                else:
                    pe.wait_ge(s.tanh_done, n)
                pe.wait_ge(s.mask_set, 2)
                for j in range(REP):
                    pe.matmul(sc_ps[:, j, 0:SC], ident_b[:], mask[:], start=True, stop=False, skip_group_check=True)
                for j in range(REP):
                    r = slice(j * D, (j + 1) * D)
                    pe.matmul(sc_ps[:, j, 0:K1], kt[r, p, g, P:S], qt[r, p, g, P:S], start=False, stop=False, skip_group_check=True, tile_position=(j * D, 0))
                for j in range(REP):
                    r = slice(j * D, (j + 1) * D)
                    mm = pe.matmul(sc_ps[:, j, K1:SC], kt[r, p, g, 0:P], qt[r, p, g, 0:K0], start=False, stop=True, skip_group_check=True, tile_position=(j * D, 0))
                mm.then_inc(s.scores_mm, 1)

            def weigh(b, p, g):
                n = b * 2 + g
                o = pv[:, 0:QT * REP * (D + 1)].rearrange("p (t h d) -> p t h d", t=QT, h=REP)
                pe.wait_ge(s.probs_done, n + 1)
                pe.wait_ge(s.pool_consts, 4)
                if g == 0:
                    pe.wait_ge(s.v_done, (b + 1) * QT)
                    if isinstance(b, int) and b == 0:
                        pe.wait_ge(s.cols_done, 2)
                    else:
                        pass
                    after(pe, s.gate_done, b - 1)
                else:
                    pe.wait_ge(s.attn_done, n)
                pe.matmul(o[:, 0], masked[:], v[:, p, 1, g].unsqueeze(1).to_broadcast([P, REP, D + 1]), start=True, stop=False, skip_group_check=True)
                for j in range(REP):
                    pe.matmul(o[:, 0, j], probs[:, g, j, P:2 * P], v[:, p, 0, g], start=False, stop=True, skip_group_check=True)
                for j in range(REP):
                    pe.matmul(o[:, 1, j], probs[:, g, j, 2 * P:3 * P], v[:, p, 0, g], start=True, stop=False, skip_group_check=True)
                    mm = pe.matmul(o[:, 1, j], probs[:, g, j, 0:P], v[:, p, 1, g], start=False, stop=True, skip_group_check=True)
                mm.then_inc(s.pv_mm, 1)

            def step(b, p, lead=False, here=False, lag=False):
                if lead:
                    turn_xhat(b + 1)
                if here:
                    scores(b, p, 0)
                if lead:
                    project(b + 1)
                if lag:
                    pe.wait_ge(s.attn_done, 2 * b)
                    if lead:
                        pe.wait_ge(s.ht_done, (b + 2) * KC)
                        pe.wait_ge(s.hth_done, (b + 2) * KC)
                    else:
                        pe.wait_ge(s.qt_done, B)
                        pe.wait_ge(s.h2t_done, b - 1)
                    for t in range(QT):
                        for c in range(KC):
                            mm = pe.transpose(tp[:, c, t * P:(t + 1) * P], attn[:, t, c * P:(c + 1) * P], ident[:])
                    mm.then_inc(s.attn_t, 1)
                if here:
                    weigh(b, p, 0)
                if lag:
                    pe.wait_ge(s.otl_done, b)
                    pe.wait_ge(s.oth_done, b)
                    pe.wait_ge(s.wol_done, 1)
                    if lead:
                        pe.wait_ge(s.qkv_done, b + 2)
                    else:
                        after(pe, s.gated_done, b - 1)
                    for t in range(QT):
                        mm = split3(qkv_ps[:, 1, t * HID:(t + 1) * HID], [oth[:, c, t * P:(t + 1) * P] for c in range(KC)],
                                    [otl[:, c, t * P:(t + 1) * P] for c in range(KC)], [woh[:, c] for c in range(KC)], [wol[:, c] for c in range(KC)])
                    mm.then_inc(s.wo_mm, 1)
                if here:
                    scores(b, p, 1)
                    weigh(b, p, 1)
                if lag:
                    pe.wait_ge(s.h2_done, b)
                    pe.wait_ge(s.otl_done, b)
                    for t in range(QT):
                        for c in range(KC):
                            mm = pe.transpose(tp[:, c, t * P:(t + 1) * P], h2b[:, t, c * P:(c + 1) * P], ident[:])
                    mm.then_inc(s.h2_t, 1)
                    pe.wait_ge(s.h2t_done, b)
                    if here:
                        pe.wait_ge(s.attn_done, 2 * b + 2)
                    else:
                        pe.wait_ge(s.gate_done, b - 1)
                    for t in range(QT):
                        for c in range(KC):
                            mm = pe.matmul(pv[:, t * E:(t + 1) * E], h2t[:, c, t * P:(t + 1) * P], wgate[:, c], start=(c == 0), stop=(c == KC - 1))
                    mm.then_inc(s.logits_mm, 1)
                if lead:
                    turn_qk(b + 1, lag)

            batches(pe, step)


def routing(nc, a, gate_t, cw):
    with ExitStack() as ctx:
        def sb(name, shape, dt=F32):
            return ctx.enter_context(nc.sbuf_tensor(name, shape, dt))

        bias = sb("bias", [P, E])
        lower = sb("lower", [P, G, G])
        iota = sb("iota", [P, E])
        sig = sb("sig", [P, NT, E])
        biased = sb("biased", [P, NT, E])
        gmax = sb("gmax", [P, NT, G])
        g_gt = sb("g_gt", [P, NT, G, G])
        g_eq = sb("g_eq", [P, NT, G, G])
        rank = sb("rank", [P, NT, G])
        gfar = sb("gfar", [P, NT, G])
        top = sb("top", [P, NT, 8])
        idx = sb("idx", [P, NT, 8], U32)
        idxf = sb("idxf", [P, NT, TOPK])
        onehot = sb("onehot", [P, NT, TOPK, E])
        picked = sb("picked", [P, NT, E])
        wsel = sb("wsel", [P, NT, E])
        wsum = sb("wsum", [P, NT])
        s = named({n: ctx.enter_context(nc.semaphore("r_" + n)) for n in
                               ("small_in sig biased gmax ggt geq geqm rank gfar maskg masked top idx idxf onehot picked wsel wsum cw").split()})
        block = ctx.enter_context(nc.Block())

        @block.sync
        def _(sp):
            for n, (dst, src) in enumerate(((bias, "bias"), (lower, "lower"), (iota, "iota"))):
                d = dst[:] if n != 1 else dst[:].rearrange("p a b -> p (a b)")
                sp.dma_start(d, a[src]).then_inc(s.small_in, 16)

        @block.vector
        def _(dve):
            dve.wait_ge(s.small_in, 48)
            n_gate = [P, NT, G, G]
            dve.tensor_scalar(sig[:], gate_t[:], 0.5, 0.5, ALU.mult, ALU.add).then_inc(s.sig, 1)
            dve.wait_ge(s.sig, 1)
            dve.tensor_tensor(biased[:], sig[:], bias[:].unsqueeze(1).to_broadcast([P, NT, E]), ALU.add).then_inc(s.biased, 1)
            dve.wait_ge(s.biased, 1)
            dve.tensor_reduce(gmax[:], biased[:].rearrange("p t (g k) -> p t g k", g=G), AX.X, ALU.max).then_inc(s.gmax, 1)
            dve.wait_ge(s.gmax, 1)
            other, own = gmax[:].unsqueeze(2).to_broadcast(n_gate), gmax[:].unsqueeze(3).to_broadcast(n_gate)
            dve.tensor_tensor(g_gt[:], other, own, ALU.is_gt).then_inc(s.ggt, 1)
            dve.tensor_tensor(g_eq[:], other, own, ALU.is_equal).then_inc(s.geq, 1)
            dve.wait_ge(s.geq, 1)
            dve.tensor_tensor(g_eq[:], g_eq[:], lower[:].unsqueeze(1).to_broadcast(n_gate), ALU.mult).then_inc(s.geqm, 1)
            dve.wait_ge(s.geqm, 1)
            dve.wait_ge(s.ggt, 1)
            dve.tensor_tensor(g_gt[:], g_gt[:], g_eq[:], ALU.add).then_inc(s.ggt, 1)
            dve.wait_ge(s.ggt, 2)
            dve.tensor_reduce(rank[:], g_gt[:], AX.X, ALU.add).then_inc(s.rank, 1)
            dve.wait_ge(s.rank, 1)
            dve.tensor_scalar(gfar[:], rank[:], float(TOPK_G), -FAR, ALU.is_ge, ALU.mult).then_inc(s.gfar, 1)
            dve.tensor_scalar(rank[:], rank[:], float(TOPK_G), None, ALU.is_lt).then_inc(s.gfar, 1)
            dve.wait_ge(s.gfar, 2)
            spread = lambda g: g[:].unsqueeze(3).to_broadcast([P, NT, G, EG])
            b4 = biased[:].rearrange("p t (g k) -> p t g k", g=G)
            dve.tensor_tensor(b4, b4, spread(rank), ALU.mult).then_inc(s.maskg, 1)
            dve.wait_ge(s.maskg, 1)
            dve.tensor_tensor(b4, b4, spread(gfar), ALU.add).then_inc(s.masked, 1)
            dve.wait_ge(s.masked, 1)
            for t in range(NT):
                dve.max(top[:, t], biased[:, t]).then_inc(s.top, 1)
            for t in range(NT):
                dve.wait_ge(s.top, t + 1)
                dve.max_index(idx[:, t], top[:, t], biased[:, t]).then_inc(s.idx, 1)
            dve.wait_ge(s.idx, NT)
            dve.tensor_copy(idxf[:], idx[:, :, 0:TOPK]).then_inc(s.idxf, 1)
            dve.wait_ge(s.idxf, 1)
            for k in range(TOPK):
                dve.tensor_tensor(onehot[:, :, k], iota[:].unsqueeze(1).to_broadcast([P, NT, E]), idxf[:, :, k:k + 1].to_broadcast([P, NT, E]),
                                  ALU.is_equal).then_inc(s.onehot, 1)
            dve.wait_ge(s.onehot, TOPK)
            dve.tensor_reduce(picked[:], onehot[:].rearrange("p t k e -> p t e k"), AX.X, ALU.add).then_inc(s.picked, 1)
            dve.wait_ge(s.picked, 1)
            dve.tensor_tensor(wsel[:], picked[:], sig[:], ALU.mult).then_inc(s.wsel, 1)
            dve.wait_ge(s.wsel, 1)
            dve.tensor_reduce(wsum[:], wsel[:], AX.X, ALU.add).then_inc(s.wsum, 1)
            dve.wait_ge(s.wsum, 1)
            dve.reciprocal(wsum[:], wsum[:]).then_inc(s.wsum, 1)
            dve.wait_ge(s.wsum, 2)
            dve.tensor_tensor(cw[:, :, 0:E], wsel[:], wsum[:].unsqueeze(2).to_broadcast([P, NT, E]), ALU.mult).then_inc(s.cw, 1)
            dve.memset(cw[:, :, E:NE], 1.0).then_inc(s.cw, 1)
            dve.wait_ge(s.cw, 2)


def ffn(nc, a, out, mod_rows, x1, h2, cw, ident):
    with ExitStack() as ctx:
        def sb(name, shape, dt=F32):
            return ctx.enter_context(nc.sbuf_tensor(name, shape, dt))

        def sem(name):
            return ctx.enter_context(nc.semaphore(name))

        w13h = sb("w13h", [P, NE, KC, 2 * INTER], F32R)
        w13l = sb("w13l", [P, NE, KC, 2 * INTER], F32R)
        w2ah = sb("w2ah", [HA, NE, HID], F32R)
        w2al = sb("w2al", [HA, NE, HID], F32R)
        w2b = sb("w2b", [P, NE, HID], F32R)
        w13_raw = sb("w13_raw", [P, KC * 2 * INTER])
        w2a_raw = sb("w2a_raw", [HA, HID])
        w2b_raw = sb("w2b_raw", [P, HID])
        w2b_r = sb("w2b_r", [P, HID], F32R)
        tick = sb("f_tick", [P, 1])
        tick_src = sb("tick_src", [P, 1])
        xb = sb("xb", [P, HID])
        xth = sb("xth", [P, KC, P], F32R)
        xtl = sb("xtl", [P, KC, P], F32R)
        silu = sb("silu", [P, 2, INTER])
        hid = sb("hid", [P, 2, HW])
        hth = sb("f_hth", [P, 2, 2, P], F32R)
        htl = sb("f_htl", [P, 2, 2, P], F32R)
        mod = sb("f_mod", [P, 1, HID])
        yg = sb("yg", [P, HID])
        yo = sb("yo", [P, 1, HID])

        up = ctx.enter_context(nc.psum_tensor("up", [P, 2, 512], F32))
        xt_ps = ctx.enter_context(nc.psum_tensor("xt_ps", [P, 512], F32))
        ht_ps = ctx.enter_context(nc.psum_tensor("ht_ps", [P, 2, 512], F32))
        y_ps = ctx.enter_context(nc.psum_tensor("y_ps", [P, 512], F32))
        s = named({n: sem("f_" + n) for n in (
            "tick raw_in raw_h raw_l mod_in xb xt xth xtl up silu hid dup ht hth htl down yg yo stored").split()})
        block = ctx.enter_context(nc.Block())

        @block.sync
        def _(sp):
            def load(e):
                if not isinstance(e, int):
                    sp.wait_ge(s.raw_l, 4 * e)
                sp.dma_start(w13_raw[:], a["w13"][bass.ds(e, 1)].rearrange("o p c -> p (o c)")).then_inc(s.raw_in, 16)
                sp.dma_start(w2a_raw[:], a["w2a"][bass.ds(e, 1)].rearrange("o p c -> p (o c)")).then_inc(s.raw_in, 16)
                sp.dma_start(w2b_raw[:], a["w2b"][bass.ds(e, 1)].rearrange("o p c -> p (o c)")).then_inc(s.raw_in, 16)

            load(0)
            with sp.Fori(1, NE) as e:
                load(e)
            def tile(t):
                after(sp, s.yg, t)
                src = mod_rows[bass.ds(t // QT, 1), 3:4].rearrange("o r h -> o (r h)").to_broadcast([P, HID])
                sp.dma_start(mod[:, 0], src).then_inc(s.mod_in, 16)
                sp.wait_ge(s.yo, t + 1)
                sp.dma_start(out[bass.ds(t, 1)].rearrange("o p h -> p (o h)"), yo[:, 0]).then_inc(s.stored, 16)
            tile(0)
            with sp.Fori(1, NT) as t:
                tile(t)
            sp.wait_ge(s.stored, 16 * NT)

        @block.gpsimd
        def _(pool):
            pool.memset(tick_src[:], 0.0).then_inc(s.tick, 1)
            pool.wait_ge(s.tick, 1)
            with pool.Fori(0, NE) as e:
                pool.wait_ge(s.raw_in, 48 * e + 48)
                d13h, d13l = (w[:, bass.ds(e, 1)].rearrange("p o c n -> p (o c n)") for w in (w13h, w13l))
                d2h, d2l, d2b = (w[:, bass.ds(e, 1)].rearrange("p o n -> p (o n)") for w in (w2ah, w2al, w2b))
                pool.tensor_copy(d13h, w13_raw[:]).then_inc(s.raw_h, 1)
                pool.tensor_copy(d2h, w2a_raw[:]).then_inc(s.raw_h, 1)
                pool.tensor_copy(w2b_r[:], w2b_raw[:]).then_inc(s.raw_h, 1)
                pool.wait_ge(s.raw_h, 3 * e + 3)
                pool.tensor_tensor(d13l, w13_raw[:], d13h.bitcast(F32), ALU.subtract).then_inc(s.raw_l, 1)
                pool.tensor_tensor(d2l, w2a_raw[:], d2h.bitcast(F32), ALU.subtract).then_inc(s.raw_l, 1)
                pool.tensor_tensor(d2b, w2b_raw[:], w2b_r[:].bitcast(F32), ALU.subtract).then_inc(s.raw_l, 1)
                pool.wait_ge(s.raw_l, 4 * e + 3)
                pool.tensor_tensor(tick[:], tick_src[:], tick_src[:], ALU.mult)
                pool.tensor_copy(w2b[0:HB, bass.ds(e, 1)].rearrange("p o n -> p (o n)"), w2b_raw[0:HB]).then_inc(s.raw_l, 1)

        @block.scalar
        def _(act):
            def silu_of(t, e):
                u = t * NE + e
                act.wait_ge(s.up, u + 1)
                after(act, s.hid, u - 1 if e else t * NE)
                act.activation(silu[:, e % 2], up[:, e % 2, 0:INTER], ACT.Silu).then_inc(s.silu, 1)

            def high(t, e):
                u = t * NE + e
                act.wait_ge(s.ht, u + 1)
                after(act, s.down, u - 1 if e else t * NE)
                act.activation(hth[:, e % 2].rearrange("p c n -> p (c n)"), ht_ps[:, e % 2, 0:2 * P], ACT.Copy).then_inc(s.hth, 1)

            def tile(t):
                act.wait_ge(s.xt, t + 1)
                after(act, s.up, t * NE)
                act.activation(xth[:].rearrange("p c n -> p (c n)"), xt_ps[:, 0:HID], ACT.Copy).then_inc(s.xth, 1)
                silu_of(t, 0)
                for e in range(NE):
                    if e + 1 < NE:
                        silu_of(t, e + 1)
                    high(t, e)

            tile(0)
            with act.Fori(1, NT) as t:
                tile(t)

        @block.vector
        def _(dve):
            def hidden(t, e):
                u = t * NE + e
                q = e % 2
                dve.wait_ge(s.silu, u + 1)
                after(dve, s.ht, u - 1 if e else t * NE)
                w = cw[:, bass.ds(t, 1), e:e + 1].rearrange("p o e -> p (o e)")
                dve.scalar_tensor_tensor(out=hid[:, q, 0:INTER], in0=silu[:, q], scalar=w, in1=up[:, q, INTER:2 * INTER], op0=ALU.mult, op1=ALU.mult)\
                    .then_inc(s.hid, 1)
                dve.wait_ge(s.hid, u + 1)
                dve.tensor_copy(hid[:, q, INTER:HW], hid[:, q, HA:INTER]).then_inc(s.dup, 1)

            def low(t, e):
                u = t * NE + e
                dve.wait_ge(s.hth, u + 1)
                after(dve, s.down, u - 1 if e else t * NE)
                dve.tensor_tensor(htl[:, e % 2].rearrange("p c n -> p (c n)"), ht_ps[:, e % 2, 0:2 * P],
                                  hth[:, e % 2].rearrange("p c n -> p (c n)").bitcast(F32), ALU.subtract).then_inc(s.htl, 1)

            def tile(t):
                after(dve, s.xt, t)
                dve.tensor_copy(xb[:], h2[:, bass.ds(t, 1)].rearrange("p o h -> p (o h)")).then_inc(s.xb, 1)
                dve.wait_ge(s.xth, t + 1)
                dve.tensor_tensor(xtl[:].rearrange("p c n -> p (c n)"), xt_ps[:, 0:HID], xth[:].rearrange("p c n -> p (c n)").bitcast(F32), ALU.subtract)\
                    .then_inc(s.xtl, 1)
                hidden(t, 0)
                for e in range(NE):
                    if e + 1 < NE:
                        hidden(t, e + 1)
                    low(t, e)
                dve.wait_ge(s.down, t * NE + NE)
                dve.wait_ge(s.mod_in, 16 * t + 16)
                dve.tensor_tensor(yg[:], y_ps[:, 0:HID], mod[:, 0], ALU.mult).then_inc(s.yg, 1)
                dve.wait_ge(s.yg, t + 1)
                after(dve, s.stored, 16 * t)
                dve.tensor_tensor(yo[:, 0], yg[:], x1[:, bass.ds(t, 1)].rearrange("p o h -> p (o h)"), ALU.add).then_inc(s.yo, 1)

            tile(0)
            with dve.Fori(1, NT) as t:
                tile(t)

        @block.tensor
        def _(pe):
            def up_mm(t, e):
                u = t * NE + e
                after(pe, s.hid, u - 1 if e else t * NE)
                after(pe, s.silu, u - 1 if e else t * NE)
                o = up[:, e % 2, 0:2 * INTER]
                for k in range(KC):
                    pe.matmul(o, xth[:, k], w13h[:, e, k], start=(k == 0), stop=False)
                    pe.matmul(o, xth[:, k], w13l[:, e, k], start=False, stop=False)
                    mm = pe.matmul(o, xtl[:, k], w13h[:, e, k], start=False, stop=(k == KC - 1))
                mm.then_inc(s.up, 1)

            def turn(t, e):
                u = t * NE + e
                pe.wait_ge(s.dup, u + 1)
                after(pe, s.htl, u - 1 if e else t * NE)
                pe.transpose(ht_ps[:, e % 2, 0:P], hid[:, e % 2, 0:P], ident[:])
                pe.transpose(ht_ps[:, e % 2, P:2 * P], hid[:, e % 2, HA:HW], ident[:]).then_inc(s.ht, 1)

            def down_mm(t, e):
                u = t * NE + e
                q = e % 2
                pe.wait_ge(s.htl, u + 1)
                o = y_ps[:, 0:HID]
                pe.matmul(o, hth[0:HA, q, 0], w2ah[:, e], start=(e == 0), stop=False)
                pe.matmul(o, hth[0:HA, q, 0], w2al[:, e], start=False, stop=False)
                pe.matmul(o, htl[0:HA, q, 0], w2ah[:, e], start=False, stop=False)
                pe.matmul(o, hth[:, q, 1], w2b[:, e], start=False, stop=False)
                pe.matmul(o, htl[:, q, 1], w2b[:, e], start=False, stop=(e == NE - 1)).then_inc(s.down, 1)

            pe.wait_ge(s.raw_l, 4 * NE)
            def tile(t):
                pe.wait_ge(s.xb, t + 1)
                after(pe, s.xtl, t)
                for c in range(KC):
                    mm = pe.transpose(xt_ps[:, c * P:(c + 1) * P], xb[:, c * P:(c + 1) * P], ident[:])
                mm.then_inc(s.xt, 1)
                pe.wait_ge(s.xtl, t + 1)
                up_mm(t, 0)
                after(pe, s.yg, t)
                for e in range(NE):
                    if e + 1 < NE:
                        up_mm(t, e + 1)
                    turn(t, e)
                    if e > 0:
                        down_mm(t, e - 1)
                down_mm(t, NE - 1)

            tile(0)
            with pe.Fori(1, NT) as t:
                tile(t)


def lay_out(i):
    f = {k: np.asarray(x) for k, x in i.items()}
    chunks = lambda w: np.ascontiguousarray(w.reshape(KC, P, -1).transpose(1, 0, 2))
    w1 = np.concatenate([f["L0_ffn_w1"], f["L0_ffn_sw1"].reshape(HID, SHARED, INTER).transpose(1, 0, 2)])
    w3 = np.concatenate([f["L0_ffn_w3"], f["L0_ffn_sw3"].reshape(HID, SHARED, INTER).transpose(1, 0, 2)])
    w2 = np.concatenate([f["L0_ffn_w2"], f["L0_ffn_sw2"].reshape(SHARED, INTER, HID)])
    w13 = np.concatenate([w1, w3], 2).reshape(NE, KC, P, 2 * INTER).transpose(0, 2, 1, 3).reshape(NE, P, KC * 2 * INTER)
    wqkv = np.concatenate([f["L0_attn_Wq"], f["L0_attn_Wk"], f["L0_attn_Wv"]]).T
    return {
        "x": f["L0_attn_hidden_states"],
        "ct": chunks(f["L0_c"].T),
        "wmod": chunks(f["L0_wmod"]),
        "wqkv": chunks(wqkv),
        "wo": chunks(f["L0_attn_Wo"].T),
        "wgate": chunks(f["L0_ffn_gate_w"].T),
        "bias": np.broadcast_to(f["L0_ffn_expert_bias"][None, :], (P, E)),
        "w13": w13,
        "w2a": w2[:, 0:HA],
        "w2b": np.concatenate([w2[:, HA:], w2[:, HA:]], 1),
        **constants(),
    }


def kernel(**inputs):
    import concourse.bacc as bacc
    from concourse.bass_utils import run_bass_kernel_spmd

    nc = bacc.Bacc("TRN2", target_bir_lowering=False, num_devices=1)
    arrays, args = {}, {}
    for name, x in lay_out(inputs).items():
        x = np.ascontiguousarray(x)
        arrays[f"in_{name}"] = x
        args[name] = nc.dram_tensor(f"in_{name}", x.shape, mybir.dt.from_np(x.dtype), kind="ExternalInput").ap()
    out = nc.dram_tensor("out", (NT, P, HID), F32, kind="ExternalOutput").ap()
    build(nc, args, out)
    r = run_bass_kernel_spmd(nc, [arrays], core_ids=[0])
    return r.results[0]["out"].reshape(B, S, HID)
```

```python
from contextlib import ExitStack

import numpy as np

import concourse.bass as bass
from concourse import mybir

ALU = mybir.AluOpType
ACT = mybir.ActivationFunctionType
AX = mybir.AxisListType
F32 = mybir.dt.float32
F32R = mybir.dt.float32r
BF16 = mybir.dt.bfloat16
U32 = mybir.dt.uint32

P = 128
B, S, HID = 8, 256, 256
QT = S // P
NT = B * QT
KC = HID // P
H, KV, D = 8, 2, 32
REP = H // KV
QKV = (H + 2 * KV) * D
NG = H + 2 * KV
WINDOW = 64
SOFTCAP = 30.0
Q_SCALE = 256.0
THETA = 1000000.0
SCORE_TO_TANH = Q_SCALE / float(np.sqrt(np.float32(D))) / SOFTCAP
MASKED_P = float(np.exp(np.float32(-SOFTCAP)))
LN_EPS, QK_EPS = 1e-5, 1e-6

E, INTER, TOPK, G, TOPK_G = 16, 176, 4, 4, 2
EG = E // G
SHARED = 2
NE = E + SHARED
HA = 112
HB = INTER - HA
HW = INTER + HB
GE = 3
SLOTS = 2 * GE
NG_E = NE // GE
UNITS = GE * NT
FAR = 1e30

K1, K0, SC = 128, 192, 320
PC = 384


def constants():
    inv = (1.0 / np.float32(THETA) ** (np.arange(0, D, 2, dtype=np.float32) / np.float32(D))).astype(np.float32)
    freqs = np.arange(S, dtype=np.float32)[:, None] * inv[None, :]
    cos, sin = np.cos(freqs).astype(np.float32), np.sin(freqs).astype(np.float32)
    rope = np.stack([np.concatenate([cos, cos], 1), np.concatenate([-sin, sin], 1)], 1)
    rope = rope.reshape(QT, P, 2, D).transpose(1, 2, 0, 3)
    lower = (np.arange(G)[None, :] < np.arange(G)[:, None]).astype(np.float32)
    key, col = np.arange(P)[:, None], np.arange(SC)[None, :]
    key, query = np.where(col < K1, key + P, key), np.where(col < K1, col + P, col - K1)
    allowed = (key <= query) & (key > query - WINDOW)
    return {
        "mask": np.where(allowed, 0.0, -1e5).astype(np.float32),
        "rope": np.ascontiguousarray(rope),
        "ident": np.eye(P, dtype=np.float32),
        "lower": np.ascontiguousarray(np.broadcast_to(lower.reshape(1, G * G), (P, G * G))),
        "iota": np.ascontiguousarray(np.broadcast_to(np.arange(E, dtype=np.float32), (P, E))),
    }


def build(nc, a, out):
    with ExitStack() as whole:
        def sb(name, shape, dt=F32, ctx=whole):
            return ctx.enter_context(nc.sbuf_tensor(name, shape, dt))

        mod_rows = nc.dram_tensor("mod_rows", [B, 4, HID], F32, kind="Internal").ap()

        x1 = sb("x1", [P, NT, HID])
        h2h = sb("h2h", [P, B, KC, S], F32R)
        h2l = sb("h2l", [P, B, KC, S], F32R)
        gate_t = sb("gate_t", [P, NT, E])
        cw = sb("cw", [P, NT, NE])
        ident = sb("ident", [P, P])
        w = named({
            "w13_raw": sb("w13_raw", [P, KC * 2 * INTER]),
            "w2a_raw": sb("w2a_raw", [HA, HID]),
            "w2b_raw": sb("w2b_raw", [P, HID]),
            "w2b_r": sb("w2b_r", [P, HID], F32R),
            "w13h": sb("w13h", [P, SLOTS, KC, 2 * INTER], F32R),
            "w13l": sb("w13l", [P, SLOTS, KC, 2 * INTER], F32R),
            "w2ah": sb("w2ah", [HA, SLOTS, HID], F32R),
            "w2al": sb("w2al", [HA, SLOTS, HID], F32R),
            "w2b": sb("w2b", [P, SLOTS, HID], F32R),
            "tick": sb("w_tick", [P, 3]),
            "tick_src": sb("w_tick_src", [P, 1]),
            "raw_in": whole.enter_context(nc.semaphore("w_raw_in")),
            "high_done": whole.enter_context(nc.semaphore("w_high_done")),
            "low_done": whole.enter_context(nc.semaphore("w_low_done")),
        })
        attention(nc, a, mod_rows, x1, h2h, h2l, gate_t, ident, w)
        routing(nc, a, gate_t, cw)
        ffn(nc, a, out, mod_rows, x1, h2h, h2l, cw, w, ident)


def load_expert(sp, a, w, e):
    after(sp, w.low_done, 4 * e)
    for dst, src in ((w.w13_raw, "w13"), (w.w2a_raw, "w2a"), (w.w2b_raw, "w2b")):
        sp.dma_start(dst[:], a[src][bass.ds(e, 1)].rearrange("o p c -> p (o c)")).then_inc(w.raw_in, 16)


def split_expert(pool, w, e, slot):
    d13h, d13l = (x[:, bass.ds(slot, 1)].rearrange("p o c n -> p (o c n)") for x in (w.w13h, w.w13l))
    d2h, d2l, d2b = (x[:, bass.ds(slot, 1)].rearrange("p o n -> p (o n)") for x in (w.w2ah, w.w2al, w.w2b))
    pool.wait_ge(w.raw_in, 48 * e + 48)
    pool.tensor_tensor(w.tick[:, 0:1], w.tick_src[:], w.tick_src[:], ALU.mult)
    pool.tensor_copy(d13h, w.w13_raw[:]).then_inc(w.high_done, 1)
    pool.tensor_copy(d2h, w.w2a_raw[:]).then_inc(w.high_done, 1)
    pool.tensor_copy(w.w2b_r[:], w.w2b_raw[:]).then_inc(w.high_done, 1)
    pool.wait_ge(w.high_done, 3 * e + 3)
    pool.tensor_tensor(d13l, w.w13_raw[:], d13h.bitcast(F32), ALU.subtract).then_inc(w.low_done, 1)
    pool.tensor_tensor(d2l, w.w2a_raw[:], d2h.bitcast(F32), ALU.subtract).then_inc(w.low_done, 1)
    pool.tensor_tensor(d2b, w.w2b_raw[:], w.w2b_r[:].bitcast(F32), ALU.subtract).then_inc(w.low_done, 1)
    pool.wait_ge(w.low_done, 4 * e + 3)
    pool.tensor_tensor(w.tick[:, 1:2], w.tick_src[:], w.tick_src[:], ALU.mult)
    pool.tensor_copy(w.w2b[0:HB, bass.ds(slot, 1)].rearrange("p o n -> p (o n)"), w.w2b_raw[0:HB]).then_inc(w.low_done, 1)


def named(semaphores):
    return type("Semaphores", (), semaphores)


def after(eng, sem, count):
    if not (isinstance(count, int) and count <= 0):
        eng.wait_ge(sem, count)


def attention(nc, a, mod_rows, x1, h2h, h2l, gate_t, ident, w):
    with ExitStack() as ctx:
        def sb(name, shape, dt=F32):
            return ctx.enter_context(nc.sbuf_tensor(name, shape, dt))

        def sem(name):
            return ctx.enter_context(nc.semaphore(name))

        wqkv = sb("wqkv", [P, KC, QKV])
        wqkvh = sb("wqkvh", [P, KC, QKV], F32R)
        wqkvl = sb("wqkvl", [P, KC, QKV], F32R)
        wo = sb("wo", [P, KC, HID])
        woh = sb("woh", [P, KC, HID], F32R)
        wol = sb("wol", [P, KC, HID], F32R)
        wgate = sb("wgate", [P, KC, E])
        rope = sb("rope", [P, 2, QT, D])
        ct = sb("ct", [P, KC, B])
        ct_tanh = sb("ct_tanh", [P, KC, B])
        ct_silu = sb("ct_silu", [P, KC, B])
        mod_cols = sb("mod_cols", [P, 4, B])
        rows = sb("rows", [B, 4, HID])
        rows_neg = sb("rows_neg", [B, 2, HID])
        rows_sign = sb("rows_sign", [B, 2, HID])
        mask_f = sb("mask_f", [P, SC])
        mask = sb("mask", [P, SC], BF16)
        ident_b = sb("ident_b", [P, P], BF16)
        masked = sb("masked", [P, P])
        minus_half = sb("minus_half", [P, 2 * NG])
        mod = sb("mod", [P, 2, 3, HID])
        stats = sb("stats", [P, QT, 6])
        mv = sb("mv", [P, QT, 2])
        veps = sb("veps", [P, QT])
        veps2 = sb("veps2", [P, QT])
        meansq = sb("meansq", [P, QT * NG])
        rstd = sb("rstd", [P, QT])
        xhat = sb("xhat", [P, QT, HID])
        ht = sb("ht", [P, KC, S])
        hth = sb("hth", [P, KC, S], F32R)
        htl = sb("htl", [P, KC, S], F32R)
        qkv = sb("qkv", [P, QT, QKV])
        rcos = sb("rcos", [P, QT, (H + KV) * D])
        rsin = sb("rsin", [P, QT, (H + KV) * D])
        sums = sb("sums", [P, QT * NG])
        squares = sb("squares", [P, QT, QKV])
        sumsq = sb("sumsq", [P, QT * NG])
        rn = sb("rn", [P, QT * NG])
        qn = sb("qn", [P, QT, H * D])
        kn = sb("kn", [P, QT, KV, REP, D])
        v = sb("v", [P, 2, QT, KV, D + 1])
        qt = sb("qt", [P, 2, KV, S])
        kt = sb("kt", [P, 2, KV, S])
        capped = sb("capped", [P, REP, SC])
        probs = sb("probs", [P, 2, REP, PC])
        assert 2 * REP * PC == KC * 6 * HID
        wmod = probs[:].rearrange("p g r c -> p (g r c)").rearrange("p (c n) -> p c n", c=KC)
        rden = sb("rden", [P, QT, REP])
        attn = sb("attn", [P, QT, H * D])
        oth = sb("oth", [P, KC, S], F32R)
        otl = sb("otl", [P, KC, S], F32R)
        gated = sb("gated", [P, QT, HID])
        stats2 = sb("stats2", [P, QT, 6])
        mv2 = sb("mv2", [P, QT, 2])
        rstd2 = sb("rstd2", [P, QT])
        xhat2 = sb("xhat2", [P, QT, HID])
        scaled2 = sb("scaled2", [P, QT, HID])
        tick = sb("tick", [P, 1])
        h2b = sb("h2b", [P, QT, HID])
        h2t = sb("h2t", [P, KC, S])

        sc_ps = ctx.enter_context(nc.psum_tensor("sc_ps", [P, REP, 512], F32))
        tp = ctx.enter_context(nc.psum_tensor("tp", [P, KC, S], F32))
        qkv_ps = ctx.enter_context(nc.psum_tensor("qkv_ps", [P, QT, 512], F32))
        pv = ctx.enter_context(nc.psum_tensor("pv", [P, 512], F32))

        s = named({n: sem(n) for n in (
            "c_in w_in wmod_in wo_in ct_tanh_done ct_silu_done cols_mm rows_mm cols_done rows_copied rows_neg_done "
            "rows_sign_done rows_sign2 rows_done rows_stored consts_set pool_consts probs_set wqkvh_done wqkvl_done woh_done wol_done "
            "stats_done mv_done var_eps rstd_done xhat_done xhat_t ht_done hth_done htl_done qkv_mm qkv_done rcos_done rsin_done "
            "rot_done sums_done centered squared sumsq_done rn_eps rn_done q_done k_done v_done q_t qt_done k_t kt_done scores_mm "
            "tanh_done mask_set probs_done pv_mm rden_done attn_done attn_t oth_done otl_done wo_mm gated_done x1_done "
            "stats2_done mv2_done var2_eps rstd2_done xhat2_done scaled2_done h2_done h2_t h2t_done h2h_done h2l_done logits_mm gate_done").split()})

        x_in = [sem(f"x_in{b}") for b in range(B // 2)]
        mod_in = [sem(f"mod_in{p}") for p in range(2)]

        block = ctx.enter_context(nc.Block())

        def batches(eng, step):
            step(-1, 1, lead=True)
            step(0, 0, lead=True, here=True)
            step(1, 1, lead=True, here=True, lag=True)
            with eng.Fori(1, B // 2 - 1) as i:
                for p in range(2):
                    step(i * 2 + p, p, lead=True, here=True, lag=True)
            step(B - 2, 0, lead=True, here=True, lag=True)
            step(B - 1, 1, here=True, lag=True)
            step(B, 0, lag=True)

        @block.sync
        def _(sp):
            sp.dma_start(ct[:], a["ct"]).then_inc(s.c_in, 16)
            sp.dma_start(wmod, a["wmod"]).then_inc(s.wmod_in, 16)

            def load_x(b):
                src = a["x"][2 * b:2 * b + 2].rearrange("b (t p) h -> p (b t) h", p=P)
                sp.dma_start(x1[:, 2 * b * QT:(2 * b + 2) * QT], src).then_inc(x_in[b], 16)

            def load_mod(b, p):
                if not (isinstance(b, int) and b < 2):
                    sp.wait_ge(s.h2_done, b - 1)
                src = mod_rows[bass.ds(b, 1), 0:3].rearrange("o r h -> o (r h)").to_broadcast([P, 3 * HID])
                sp.dma_start(mod[:, p].rearrange("p r h -> p (r h)"), src).then_inc(mod_in[p], 16)

            load_x(0)
            load_expert(sp, a, w, 0)
            sp.dma_start(ident[:], a["ident"]).then_inc(s.w_in, 16)
            sp.dma_start(wqkv[:], a["wqkv"]).then_inc(s.w_in, 16)
            sp.dma_start(rope[:], a["rope"]).then_inc(s.w_in, 16)
            sp.dma_start(mask_f[:], a["mask"]).then_inc(s.w_in, 16)
            sp.dma_start(wo[:], a["wo"]).then_inc(s.wo_in, 16)
            sp.dma_start(wgate[:], a["wgate"]).then_inc(s.wo_in, 16)
            for b in range(1, B // 2):
                load_x(b)
            sp.wait_ge(s.rows_done, 2)
            sp.dma_start(mod_rows.rearrange("b r h -> b (r h)"), rows[:].rearrange("b r h -> b (r h)")).then_inc(s.rows_stored, 16)
            sp.wait_ge(s.rows_stored, 16)
            load_mod(0, 0)
            load_mod(1, 1)
            with sp.Fori(1, B // 2) as i:
                for p in range(2):
                    load_expert(sp, a, w, i * 2 + p - 1)
                    load_mod(i * 2 + p, p)

        @block.gpsimd
        def _(pool):
            pool.memset(minus_half[:], -0.5).then_inc(s.pool_consts, 1)
            pool.memset(masked[:], MASKED_P).then_inc(s.pool_consts, 1)
            pool.memset(v[:, :, :, :, D:D + 1], 1.0).then_inc(s.pool_consts, 1)
            pool.memset(w.tick_src[:], 0.0).then_inc(s.pool_consts, 1)

            def first_rstd(b):
                pool.wait_ge(s.var_eps, b + 1)
                pool.tensor_tensor(rstd[:], veps[:], minus_half[:, 0:QT], ALU.pow).then_inc(s.rstd_done, 1)

            def rotate_sin(b):
                pool.wait_ge(s.qkv_done, b + 1)
                after(pool, s.rot_done, b)
                half = D // 2
                for t in range(QT):
                    src = qkv[:, t, 0:(H + KV) * D].rearrange("p (g d) -> p g d", d=D)
                    dst = rsin[:, t].rearrange("p (g d) -> p g d", d=D)
                    for lo, frm in ((0, half), (half, 0)):
                        tab = rope[:, 1, t, lo:lo + half].unsqueeze(1).to_broadcast([P, H + KV, half])
                        pool.tensor_tensor(dst[:, :, lo:lo + half], src[:, :, frm:frm + half], tab, ALU.mult).then_inc(s.rsin_done, 1)

            def group_rstd(b):
                pool.wait_ge(s.rn_eps, b + 1)
                pool.tensor_tensor(rn[:], meansq[:], minus_half[:], ALU.pow).then_inc(s.rn_done, 1)

            def normed_v(b, p):
                after(pool, s.pv_mm, 2 * b - 2)
                pool.wait_ge(s.rn_done, b + 1)
                for t in range(QT):
                    pool.tensor_tensor(
                        v[:, p, t, :, 0:D], qkv[:, t, (H + KV) * D:].rearrange("p (g d) -> p g d", d=D),
                        rn[:, t * NG + H + KV:(t + 1) * NG].unsqueeze(2).to_broadcast([P, KV, D]), ALU.mult).then_inc(s.v_done, 1)

            def step(b, p, lead=False, here=False, lag=False):
                if lead and isinstance(b, int) and b < 0:
                    pool.wait_ge(s.pool_consts, 4)
                    first_rstd(0)
                    pool.wait_ge(s.w_in, 64)
                if lead:
                    rotate_sin(b + 1)
                if lag:
                    pool.wait_ge(s.var2_eps, b)
                    pool.tensor_tensor(rstd2[:], veps2[:], minus_half[:, 0:QT], ALU.pow).then_inc(s.rstd2_done, 1)
                if lead:
                    group_rstd(b + 1)
                    normed_v(b + 1, 1 - p)
                    if not (isinstance(b, int) and b == B - 2):
                        first_rstd(b + 2)
                if isinstance(b, int) and b < 0:
                    pool.wait_ge(s.cols_mm, 1)
                    pool.wait_ge(s.rows_mm, 1)
                    pool.memset(probs[:, :, :, SC:PC], MASKED_P).then_inc(s.probs_set, 1)
                if lag:
                    pool.wait_ge(s.h2t_done, b)
                    pool.wait_ge(s.h2h_done, b)
                    high, low = (x[:, bass.ds(b - 1, 1)].rearrange("p o c q -> p (o c q)") for x in (h2h, h2l))
                    pool.tensor_tensor(low, h2t[:].rearrange("p c q -> p (c q)"), high.bitcast(F32), ALU.subtract).then_inc(s.h2l_done, 1)
                if here and not (isinstance(b, int) and b >= SLOTS):
                    split_expert(pool, w, b, b)

            batches(pool, step)

        @block.scalar
        def _(act):
            act.wait_ge(s.c_in, 16)
            act.activation(ct_tanh[:], ct[:], ACT.Tanh, scale=0.5).then_inc(s.ct_tanh_done, 1)
            act.wait_ge(s.w_in, 64)
            act.activation(wqkvh[:], wqkv[:], ACT.Copy).then_inc(s.wqkvh_done, 1)
            act.wait_ge(s.cols_done, 2)

            def modulated(b):
                act.wait_ge(s.xhat_t, b + 1)
                after(act, s.htl_done, b)
                after(act, s.qkv_mm, b)
                for c in range(KC):
                    scale, shift = (mod_cols[:, 2 * r + c, bass.ds(b, 1)] for r in (1, 0))
                    act.activation(ht[:, c], tp[:, c], ACT.Identity, scale=scale, bias=shift).then_inc(s.ht_done, 1)
                    act.activation(hth[:, c], tp[:, c], ACT.Identity, scale=scale, bias=shift).then_inc(s.hth_done, 1)

            def copy_qkv(b):
                act.wait_ge(s.qkv_mm, b + 1)
                after(act, s.q_done, b)
                after(act, s.k_done, b * QT * KV)
                after(act, s.v_done, b * QT)
                act.activation(qkv[:], qkv_ps[:, :, 0:QKV], ACT.Copy).then_inc(s.qkv_done, 1)

            def square(b):
                act.wait_ge(s.centered, b + 1)
                after(act, s.sumsq_done, b)
                act.activation(squares[:], qkv[:], ACT.Square).then_inc(s.squared, 1)

            def copy_qkt(b, p):
                after(act, s.scores_mm, 2 * b - 2)
                act.wait_ge(s.k_t, b + 1)
                act.activation(kt[:, p].rearrange("p g q -> p (g q)"), qkv_ps[:, 0, :], ACT.Copy).then_inc(s.kt_done, 1)
                act.wait_ge(s.q_t, b + 1)
                act.activation(qt[:, p], tp[:], ACT.Copy).then_inc(s.qt_done, 1)

            def cap(b, g):
                n = b * 2 + g
                act.wait_ge(s.scores_mm, n + 1)
                after(act, s.probs_done, n)
                act.activation(capped[:], sc_ps[:, :, 0:SC], ACT.Tanh, scale=SCORE_TO_TANH).then_inc(s.tanh_done, 1)

            def exps(b, g):
                n = b * 2 + g
                act.wait_ge(s.tanh_done, n + 1)
                act.wait_ge(s.pool_consts, 4)
                act.wait_ge(s.probs_set, 1)
                after(act, s.pv_mm, 2 * b)
                act.activation(probs[:, g, :, 0:SC], capped[:], ACT.Exp, scale=SOFTCAP).then_inc(s.probs_done, 1)

            def step(b, p, lead=False, here=False, lag=False):
                if lead:
                    modulated(b + 1)
                if isinstance(b, int) and b < 0:
                    act.activation(mask[:], mask_f[:], ACT.Copy).then_inc(s.mask_set, 1)
                    act.activation(ident_b[:], ident[:], ACT.Copy).then_inc(s.mask_set, 1)
                    act.wait_ge(s.wo_in, 32)
                    act.activation(woh[:], wo[:], ACT.Copy).then_inc(s.woh_done, 1)
                if here:
                    cap(b, 0)
                    exps(b, 0)
                if lead:
                    copy_qkv(b + 1)
                if lag:
                    act.wait_ge(s.attn_t, b)
                    after(act, s.wo_mm, b - 1)
                    act.activation(oth[:], tp[:], ACT.Copy).then_inc(s.oth_done, 1)
                if here:
                    cap(b, 1)
                if lead:
                    square(b + 1)
                if isinstance(b, int) and b < 0:
                    act.wait_ge(s.rows_mm, 1)
                    act.activation(rows[:].rearrange("b r h -> b (r h)")[:, 0:512], sc_ps[0:B, 0, :], ACT.Copy).then_inc(s.rows_copied, 1)
                    act.activation(rows[:].rearrange("b r h -> b (r h)")[:, 512:1024], sc_ps[0:B, 1, :], ACT.Copy).then_inc(s.rows_copied, 1)
                if here:
                    exps(b, 1)
                if lag:
                    act.wait_ge(s.h2_t, b)
                    after(act, s.logits_mm, b - 1)
                    after(act, s.h2l_done, b - 1)
                    act.activation(h2t[:], tp[:], ACT.Copy).then_inc(s.h2t_done, 1)
                    act.activation(h2h[:, bass.ds(b - 1, 1)].rearrange("p o c q -> p (o c q)"), tp[:].rearrange("p c q -> p (c q)"),
                                   ACT.Copy).then_inc(s.h2h_done, 1)
                if lead:
                    copy_qkt(b + 1, 1 - p)
                if lag:
                    act.wait_ge(s.logits_mm, b)
                    act.activation(gate_t[:, bass.ds(b * 2 - 2, QT)], pv[:, 0:QT * E].rearrange("p (t e) -> p t e", e=E),
                                   ACT.Tanh, scale=0.5).then_inc(s.gate_done, 1)

            batches(act, step)

        @block.vector
        def _(dve):
            def gate_dve():
                dve.memset(tick[:], 0.0)

            dve.wait_ge(s.ct_tanh_done, 1)
            dve.tensor_scalar(ct_tanh[:], ct_tanh[:], 0.5, 0.5, ALU.mult, ALU.add).then_inc(s.consts_set, 1)
            dve.wait_ge(s.consts_set, 1)
            dve.tensor_tensor(ct_silu[:], ct_tanh[:], ct[:], ALU.mult).then_inc(s.ct_silu_done, 1)
            dve.wait_ge(s.cols_mm, 1)
            cols = pv[:, 0:4 * B].rearrange("p (m b) -> p m b", b=B)
            dve.tensor_copy(mod_cols[:, 0:2], cols[:, 0:2]).then_inc(s.cols_done, 1)
            dve.tensor_scalar(mod_cols[:, 2:4], cols[:, 2:4], 1.0, None, ALU.add).then_inc(s.cols_done, 1)

            def layernorm1_stats(b):
                if isinstance(b, int):
                    if b % 2 == 0:
                        dve.wait_ge(x_in[b // 2], 16)
                        gate_dve()
                else:
                    for n in range(1, B // 2):
                        dve.wait_ge(x_in[n], 16)
                    gate_dve()
                for t in range(QT):
                    dve.bn_stats(stats[:, t], x1[:, bass.ds(b * 2 + t, 1)]).then_inc(s.stats_done, 1)
                dve.wait_ge(s.stats_done, 2 * b + 2)
                gate_dve()
                for t in range(QT):
                    dve.bn_aggr(mv[:, t], stats[:, t]).then_inc(s.mv_done, 1)
                dve.wait_ge(s.mv_done, 2 * b + 2)
                dve.tensor_scalar(veps[:], mv[:, :, 1], LN_EPS, None, ALU.add).then_inc(s.var_eps, 1)

            def layernorm1_apply(b):
                after(dve, s.xhat_t, b)
                dve.wait_ge(s.rstd_done, b + 1)
                for t in range(QT):
                    dve.tensor_scalar(xhat[:, t], x1[:, bass.ds(b * 2 + t, 1)].rearrange("p o h -> p (o h)"), mv[:, t, 0:1], rstd[:, t:t + 1],
                                      ALU.subtract, ALU.mult).then_inc(s.xhat_done, 1)

            def rotate_cos(b):
                dve.wait_ge(s.qkv_done, b + 1)
                for t in range(QT):
                    tab = rope[:, 0, t].unsqueeze(1).to_broadcast([P, H + KV, D])
                    dve.tensor_tensor(rcos[:, t].rearrange("p (g d) -> p g d", d=D), qkv[:, t, 0:(H + KV) * D].rearrange("p (g d) -> p g d", d=D),
                                      tab, ALU.mult).then_inc(s.rcos_done, 1)

            groups = qkv[:].rearrange("p t (g d) -> p (t g) d", d=D)

            def centre(b):
                dve.wait_ge(s.rcos_done, (b + 1) * QT)
                dve.wait_ge(s.rsin_done, (b + 1) * 2 * QT)
                dve.tensor_tensor(qkv[:, :, 0:(H + KV) * D], rcos[:], rsin[:], ALU.add).then_inc(s.rot_done, 1)
                dve.wait_ge(s.rot_done, b + 1)
                dve.tensor_reduce(sums[:], groups, AX.X, ALU.add).then_inc(s.sums_done, 1)
                dve.wait_ge(s.sums_done, b + 1)
                dve.scalar_tensor_tensor(out=groups, in0=sums[:].unsqueeze(2).to_broadcast([P, QT * NG, D]), scalar=-1.0 / D, in1=groups,
                                         op0=ALU.mult, op1=ALU.add).then_inc(s.centered, 1)

            def mean_square(b):
                dve.wait_ge(s.squared, b + 1)
                dve.tensor_reduce(sumsq[:], squares[:].rearrange("p t (g d) -> p (t g) d", d=D), AX.X, ALU.add).then_inc(s.sumsq_done, 1)
                dve.wait_ge(s.sumsq_done, b + 1)
                dve.tensor_scalar(meansq[:], sumsq[:], 1.0 / D, QK_EPS, ALU.mult, ALU.add).then_inc(s.rn_eps, 1)

            def normed_q(b):
                dve.wait_ge(s.rn_done, b + 1)
                after(dve, s.q_t, b)
                dve.tensor_tensor(qn[:].rearrange("p t (g d) -> p t g d", d=D), qkv[:, :, 0:H * D].rearrange("p t (g d) -> p t g d", d=D),
                                  rn[:].rearrange("p (t g) -> p t g", g=NG)[:, :, 0:H].unsqueeze(3).to_broadcast([P, QT, H, D]),
                                  ALU.mult).then_inc(s.q_done, 1)

            def normed_k(b):
                after(dve, s.k_t, b)
                for t in range(QT):
                    for c in range(KV):
                        dve.tensor_scalar(kn[:, t, c], qkv[:, t, (H + c) * D:(H + c + 1) * D].unsqueeze(1).to_broadcast([P, REP, D]),
                                          rn[:, t * NG + H + c:t * NG + H + c + 1], None, ALU.mult).then_inc(s.k_done, 1)

            def normalise(b, g):
                n = b * 2 + g
                dve.wait_ge(s.pv_mm, n + 1)
                o = pv[:, 0:QT * REP * (D + 1)].rearrange("p (t h d) -> p t h d", t=QT, h=REP)
                after(dve, s.attn_done, n)
                dve.reciprocal(rden[:].unsqueeze(3), o[:, :, :, D:D + 1]).then_inc(s.rden_done, 1)
                if g == 0:
                    after(dve, s.attn_t, b)
                dve.wait_ge(s.rden_done, n + 1)
                dve.tensor_tensor(attn[:, :, g * REP * D:(g + 1) * REP * D].rearrange("p t (h d) -> p t h d", d=D), o[:, :, :, 0:D],
                                  rden[:].unsqueeze(3).to_broadcast([P, QT, REP, D]), ALU.mult).then_inc(s.attn_done, 1)

            def residual(b, p):
                dve.wait_ge(s.wo_mm, b + 1)
                dve.wait_ge(mod_in[p], 8 * (b - p) + 16)
                dve.tensor_tensor(gated[:], qkv_ps[:, 1].rearrange("p (t h) -> p t h", t=QT), mod[:, p, 0:1].to_broadcast([P, QT, HID]), ALU.mult)\
                    .then_inc(s.gated_done, 1)
                dve.wait_ge(s.gated_done, b + 1)
                x1_b = x1[:, bass.ds(b * 2, QT)]
                dve.tensor_tensor(x1_b, gated[:], x1_b, ALU.add).then_inc(s.x1_done, 1)

            def layernorm2(b):
                dve.wait_ge(s.x1_done, b + 1)
                gate_dve()
                for t in range(QT):
                    dve.bn_stats(stats2[:, t], x1[:, bass.ds(b * 2 + t, 1)]).then_inc(s.stats2_done, 1)
                dve.wait_ge(s.stats2_done, 2 * b + 2)
                gate_dve()
                for t in range(QT):
                    dve.bn_aggr(mv2[:, t], stats2[:, t]).then_inc(s.mv2_done, 1)
                dve.wait_ge(s.mv2_done, 2 * b + 2)
                dve.tensor_scalar(veps2[:], mv2[:, :, 1], LN_EPS, None, ALU.add).then_inc(s.var2_eps, 1)

            def normed2(b):
                after(dve, s.scaled2_done, b)
                dve.wait_ge(s.rstd2_done, b + 1)
                for t in range(QT):
                    dve.tensor_scalar(xhat2[:, t], x1[:, bass.ds(b * 2 + t, 1)].rearrange("p o h -> p (o h)"), mv2[:, t, 0:1], rstd2[:, t:t + 1],
                                      ALU.subtract, ALU.mult).then_inc(s.xhat2_done, 1)

            def modulate(b, p):
                dve.wait_ge(s.xhat2_done, (b + 1) * QT)
                dve.tensor_tensor(scaled2[:], xhat2[:], mod[:, p, 2:3].to_broadcast([P, QT, HID]), ALU.mult).then_inc(s.scaled2_done, 1)
                dve.wait_ge(s.scaled2_done, b + 1)
                after(dve, s.h2_t, b)
                dve.tensor_tensor(h2b[:], scaled2[:], mod[:, p, 1:2].to_broadcast([P, QT, HID]), ALU.add).then_inc(s.h2_done, 1)

            def step(b, p, lead=False, here=False, lag=False):
                if lead:
                    if isinstance(b, int) and b < 0:
                        layernorm1_stats(0)
                        layernorm1_apply(0)
                    dve.wait_ge(s.wqkvh_done, 1)
                    dve.tensor_tensor(wqkvl[:], wqkv[:], wqkvh[:].bitcast(F32), ALU.subtract).then_inc(s.wqkvl_done, 1)
                    dve.wait_ge(s.ht_done, (b + 2) * KC)
                    dve.wait_ge(s.hth_done, (b + 2) * KC)
                    after(dve, s.qkv_mm, b + 1)
                    dve.tensor_tensor(htl[:], ht[:], hth[:].bitcast(F32), ALU.subtract).then_inc(s.htl_done, 1)
                if lead:
                    rotate_cos(b + 1)
                if lag:
                    dve.wait_ge(s.oth_done, b)
                    after(dve, s.wo_mm, b - 1)
                    dve.tensor_tensor(otl[:], tp[:], oth[:].bitcast(F32), ALU.subtract).then_inc(s.otl_done, 1)
                if lead:
                    centre(b + 1)
                if lag:
                    residual(b - 1, 1 - p)
                    layernorm2(b - 1)
                if lead:
                    mean_square(b + 1)
                if isinstance(b, int) and b < 0:
                    dve.wait_ge(s.rows_copied, 2)
                    dve.tensor_scalar(rows[:, 2], rows[:, 2], 1.0, None, ALU.add).then_inc(s.rows_done, 1)
                    gates = rows[:, 0:4:3]
                    dve.tensor_scalar(rows_neg[:], gates, -1.0, None, ALU.mult).then_inc(s.rows_neg_done, 1)
                    dve.tensor_scalar(rows_sign[:], gates, 0.0, None, ALU.is_ge).then_inc(s.rows_sign_done, 1)
                    dve.wait_ge(s.rows_neg_done, 1)
                    dve.tensor_tensor(rows_neg[:], rows_neg[:], gates, ALU.max).then_inc(s.rows_neg_done, 1)
                    dve.wait_ge(s.rows_sign_done, 1)
                    dve.tensor_scalar(rows_sign[:], rows_sign[:], 2.0, -1.0, ALU.mult, ALU.add).then_inc(s.rows_sign_done, 1)
                    dve.wait_ge(s.rows_neg_done, 2)
                    dve.wait_ge(s.rows_sign_done, 2)
                    dve.scalar_tensor_tensor(out=gates, in0=rows_neg[:], scalar=0.25, in1=rows_sign[:], op0=ALU.max, op1=ALU.mult).then_inc(s.rows_done, 1)
                    dve.wait_ge(s.woh_done, 1)
                    dve.tensor_tensor(wol[:], wo[:], woh[:].bitcast(F32), ALU.subtract).then_inc(s.wol_done, 1)
                if lag:
                    normed2(b - 1)
                    modulate(b - 1, 1 - p)
                if here:
                    normalise(b, 0)
                if lead:
                    if not (isinstance(b, int) and b == B - 2):
                        layernorm1_stats(b + 2)
                    normed_q(b + 1)
                    normed_k(b + 1)
                    if not (isinstance(b, int) and b == B - 2):
                        layernorm1_apply(b + 2)
                if here:
                    normalise(b, 1)

            batches(dve, step)

        @block.tensor
        def _(pe):
            pe.wait_ge(s.ct_silu_done, 1)
            pe.wait_ge(s.wmod_in, 16)
            for m in range(4):
                for k in range(KC):
                    mm = pe.matmul(pv[:, m * B:(m + 1) * B], wmod[:, k, m * P:(m + 1) * P], ct_silu[:, k], start=(k == 0), stop=(k == KC - 1))
            mm.then_inc(s.cols_mm, 1)

            def split3(out_ap, xh, xl, wh, wl):
                n = len(xh)
                for k in range(n):
                    pe.matmul(out_ap, xh[k], wh[k], start=(k == 0), stop=False)
                    pe.matmul(out_ap, xh[k], wl[k], start=False, stop=False)
                    mm = pe.matmul(out_ap, xl[k], wh[k], start=False, stop=(k == n - 1))
                return mm

            def turn_xhat(b):
                pe.wait_ge(s.xhat_done, (b + 1) * QT)
                if isinstance(b, int) and b == 0:
                    pe.wait_ge(s.w_in, 64)
                else:
                    pe.wait_ge(s.qt_done, b)
                for t in range(QT):
                    for c in range(KC):
                        mm = pe.transpose(tp[:, c, t * P:(t + 1) * P], xhat[:, t, c * P:(c + 1) * P], ident[:])
                mm.then_inc(s.xhat_t, 1)

            def project(b):
                pe.wait_ge(s.htl_done, b + 1)
                pe.wait_ge(s.hth_done, (b + 1) * KC)
                if isinstance(b, int) and b == 0:
                    pe.wait_ge(s.wqkvl_done, 1)
                else:
                    pe.wait_ge(s.kt_done, b)
                    after(pe, s.gated_done, b - 2)
                for t in range(QT):
                    mm = split3(qkv_ps[:, t, 0:QKV], [hth[:, c, t * P:(t + 1) * P] for c in range(KC)], [htl[:, c, t * P:(t + 1) * P] for c in range(KC)],
                                [wqkvh[:, c] for c in range(KC)], [wqkvl[:, c] for c in range(KC)])
                mm.then_inc(s.qkv_mm, 1)

            def turn_qk(b, lag):
                pe.wait_ge(s.k_done, (b + 1) * QT * KV)
                pe.wait_ge(s.qkv_done, b + 1)
                for t in range(QT):
                    for c in range(KV):
                        mm = pe.transpose(qkv_ps[:, 0, c * S + t * P:c * S + (t + 1) * P], kn[:, t, c].rearrange("p r d -> p (r d)"), ident[:])
                mm.then_inc(s.k_t, 1)
                pe.wait_ge(s.q_done, b + 1)
                pe.wait_ge(s.ht_done, (b + 1) * KC)
                pe.wait_ge(s.hth_done, (b + 1) * KC)
                if lag:
                    pe.wait_ge(s.h2t_done, b - 1)
                    pe.wait_ge(s.h2h_done, b - 1)
                for t in range(QT):
                    for c in range(KV):
                        mm = pe.transpose(tp[:, c, t * P:(t + 1) * P], qn[:, t, c * P:(c + 1) * P], ident[:])
                mm.then_inc(s.q_t, 1)

            def scores(b, p, g):
                n = b * 2 + g
                if g == 0:
                    pe.wait_ge(s.qt_done, b + 1)
                    pe.wait_ge(s.kt_done, b + 1)
                if isinstance(b, int) and n == 0:
                    pe.wait_ge(s.rows_copied, 2)
                else:
                    pe.wait_ge(s.tanh_done, n)
                pe.wait_ge(s.mask_set, 2)
                for j in range(REP):
                    pe.matmul(sc_ps[:, j, 0:SC], ident_b[:], mask[:], start=True, stop=False, skip_group_check=True)
                for j in range(REP):
                    r = slice(j * D, (j + 1) * D)
                    pe.matmul(sc_ps[:, j, 0:K1], kt[r, p, g, P:S], qt[r, p, g, P:S], start=False, stop=False, skip_group_check=True, tile_position=(j * D, 0))
                for j in range(REP):
                    r = slice(j * D, (j + 1) * D)
                    mm = pe.matmul(sc_ps[:, j, K1:SC], kt[r, p, g, 0:P], qt[r, p, g, 0:K0], start=False, stop=True, skip_group_check=True, tile_position=(j * D, 0))
                mm.then_inc(s.scores_mm, 1)

            def weigh(b, p, g):
                n = b * 2 + g
                o = pv[:, 0:QT * REP * (D + 1)].rearrange("p (t h d) -> p t h d", t=QT, h=REP)
                pe.wait_ge(s.probs_done, n + 1)
                pe.wait_ge(s.pool_consts, 4)
                pe.wait_ge(s.probs_set, 1)
                if g == 0:
                    pe.wait_ge(s.v_done, (b + 1) * QT)
                    if isinstance(b, int) and b == 0:
                        pe.wait_ge(s.cols_done, 2)
                    after(pe, s.gate_done, b - 1)
                else:
                    pe.wait_ge(s.attn_done, n)
                pe.matmul(o[:, 0], masked[:], v[:, p, 1, g].unsqueeze(1).to_broadcast([P, REP, D + 1]), start=True, stop=False, skip_group_check=True)
                for j in range(REP):
                    pe.matmul(o[:, 0, j], probs[:, g, j, P:2 * P], v[:, p, 0, g], start=False, stop=True, skip_group_check=True)
                for j in range(REP):
                    pe.matmul(o[:, 1, j], probs[:, g, j, 2 * P:3 * P], v[:, p, 0, g], start=True, stop=False, skip_group_check=True)
                    mm = pe.matmul(o[:, 1, j], probs[:, g, j, 0:P], v[:, p, 1, g], start=False, stop=True, skip_group_check=True)
                mm.then_inc(s.pv_mm, 1)

            def step(b, p, lead=False, here=False, lag=False):
                if lead:
                    turn_xhat(b + 1)
                if here:
                    scores(b, p, 0)
                if lead:
                    project(b + 1)
                if isinstance(b, int) and b < 0:
                    for m in range(2):
                        for k in range(KC):
                            mm = pe.matmul(sc_ps[0:B, m], ct_silu[:, k], wmod[:, k, 512 + m * 512:1024 + m * 512], start=(k == 0), stop=(k == KC - 1))
                    mm.then_inc(s.rows_mm, 1)
                if lag:
                    pe.wait_ge(s.attn_done, 2 * b)
                    if lead:
                        pe.wait_ge(s.ht_done, (b + 2) * KC)
                        pe.wait_ge(s.hth_done, (b + 2) * KC)
                    else:
                        pe.wait_ge(s.qt_done, B)
                        pe.wait_ge(s.h2t_done, b - 1)
                        pe.wait_ge(s.h2h_done, b - 1)
                    for t in range(QT):
                        for c in range(KC):
                            mm = pe.transpose(tp[:, c, t * P:(t + 1) * P], attn[:, t, c * P:(c + 1) * P], ident[:])
                    mm.then_inc(s.attn_t, 1)
                if here:
                    scores(b, p, 1)
                if lag:
                    pe.wait_ge(s.otl_done, b)
                    pe.wait_ge(s.oth_done, b)
                    pe.wait_ge(s.wol_done, 1)
                    if lead:
                        pe.wait_ge(s.qkv_done, b + 2)
                    else:
                        after(pe, s.gated_done, b - 1)
                    for t in range(QT):
                        mm = split3(qkv_ps[:, 1, t * HID:(t + 1) * HID], [oth[:, c, t * P:(t + 1) * P] for c in range(KC)],
                                    [otl[:, c, t * P:(t + 1) * P] for c in range(KC)], [woh[:, c] for c in range(KC)], [wol[:, c] for c in range(KC)])
                    mm.then_inc(s.wo_mm, 1)
                if here:
                    weigh(b, p, 0)
                    weigh(b, p, 1)
                if lag:
                    pe.wait_ge(s.h2_done, b)
                    pe.wait_ge(s.otl_done, b)
                    for t in range(QT):
                        for c in range(KC):
                            mm = pe.transpose(tp[:, c, t * P:(t + 1) * P], h2b[:, t, c * P:(c + 1) * P], ident[:])
                    mm.then_inc(s.h2_t, 1)
                if lead:
                    turn_qk(b + 1, lag)
                if lag:
                    pe.wait_ge(s.h2t_done, b)
                    if here:
                        pe.wait_ge(s.attn_done, 2 * b + 2)
                    else:
                        pe.wait_ge(s.gate_done, b - 1)
                    for t in range(QT):
                        for c in range(KC):
                            mm = pe.matmul(pv[:, t * E:(t + 1) * E], h2t[:, c, t * P:(t + 1) * P], wgate[:, c], start=(c == 0), stop=(c == KC - 1))
                    mm.then_inc(s.logits_mm, 1)

            batches(pe, step)


def routing(nc, a, gate_t, cw):
    with ExitStack() as ctx:
        def sb(name, shape, dt=F32):
            return ctx.enter_context(nc.sbuf_tensor(name, shape, dt))

        bias = sb("bias", [P, E])
        lower = sb("lower", [P, G, G])
        iota = sb("iota", [P, E])
        sig = sb("sig", [P, NT, E])
        biased = sb("biased", [P, NT, E])
        gmax = sb("gmax", [P, NT, G])
        g_gt = sb("g_gt", [P, NT, G, G])
        g_eq = sb("g_eq", [P, NT, G, G])
        rank = sb("rank", [P, NT, G])
        gfar = sb("gfar", [P, NT, G])
        top = sb("top", [P, NT, 8])
        idx = sb("idx", [P, NT, 8], U32)
        idxf = sb("idxf", [P, NT, TOPK])
        onehot = sb("onehot", [P, NT, TOPK, E])
        picked = sb("picked", [P, NT, E])
        wsel = sb("wsel", [P, NT, E])
        wsum = sb("wsum", [P, NT])
        s = named({n: ctx.enter_context(nc.semaphore("r_" + n)) for n in
                               ("small_in sig biased gmax ggt geq geqm rank gfar maskg masked top idx idxf onehot picked wsel wsum cw").split()})
        block = ctx.enter_context(nc.Block())

        @block.sync
        def _(sp):
            for n, (dst, src) in enumerate(((bias, "bias"), (lower, "lower"), (iota, "iota"))):
                d = dst[:] if n != 1 else dst[:].rearrange("p a b -> p (a b)")
                sp.dma_start(d, a[src]).then_inc(s.small_in, 16)

        @block.vector
        def _(dve):
            dve.wait_ge(s.small_in, 48)
            n_gate = [P, NT, G, G]
            dve.tensor_scalar(sig[:], gate_t[:], 0.5, 0.5, ALU.mult, ALU.add).then_inc(s.sig, 1)
            dve.wait_ge(s.sig, 1)
            dve.tensor_tensor(biased[:], sig[:], bias[:].unsqueeze(1).to_broadcast([P, NT, E]), ALU.add).then_inc(s.biased, 1)
            dve.wait_ge(s.biased, 1)
            dve.tensor_reduce(gmax[:], biased[:].rearrange("p t (g k) -> p t g k", g=G), AX.X, ALU.max).then_inc(s.gmax, 1)
            dve.wait_ge(s.gmax, 1)
            other, own = gmax[:].unsqueeze(2).to_broadcast(n_gate), gmax[:].unsqueeze(3).to_broadcast(n_gate)
            dve.tensor_tensor(g_gt[:], other, own, ALU.is_gt).then_inc(s.ggt, 1)
            dve.tensor_tensor(g_eq[:], other, own, ALU.is_equal).then_inc(s.geq, 1)
            dve.wait_ge(s.geq, 1)
            dve.tensor_tensor(g_eq[:], g_eq[:], lower[:].unsqueeze(1).to_broadcast(n_gate), ALU.mult).then_inc(s.geqm, 1)
            dve.wait_ge(s.geqm, 1)
            dve.wait_ge(s.ggt, 1)
            dve.tensor_tensor(g_gt[:], g_gt[:], g_eq[:], ALU.add).then_inc(s.ggt, 1)
            dve.wait_ge(s.ggt, 2)
            dve.tensor_reduce(rank[:], g_gt[:], AX.X, ALU.add).then_inc(s.rank, 1)
            dve.wait_ge(s.rank, 1)
            dve.tensor_scalar(gfar[:], rank[:], float(TOPK_G), -FAR, ALU.is_ge, ALU.mult).then_inc(s.gfar, 1)
            dve.tensor_scalar(rank[:], rank[:], float(TOPK_G), None, ALU.is_lt).then_inc(s.gfar, 1)
            dve.wait_ge(s.gfar, 2)
            spread = lambda g: g[:].unsqueeze(3).to_broadcast([P, NT, G, EG])
            b4 = biased[:].rearrange("p t (g k) -> p t g k", g=G)
            dve.tensor_tensor(b4, b4, spread(rank), ALU.mult).then_inc(s.maskg, 1)
            dve.wait_ge(s.maskg, 1)
            dve.tensor_tensor(b4, b4, spread(gfar), ALU.add).then_inc(s.masked, 1)
            dve.wait_ge(s.masked, 1)
            for t in range(NT):
                dve.max(top[:, t], biased[:, t]).then_inc(s.top, 1)
            for t in range(NT):
                dve.wait_ge(s.top, t + 1)
                dve.max_index(idx[:, t], top[:, t], biased[:, t]).then_inc(s.idx, 1)
            dve.wait_ge(s.idx, NT)
            dve.tensor_copy(idxf[:], idx[:, :, 0:TOPK]).then_inc(s.idxf, 1)
            dve.wait_ge(s.idxf, 1)
            for k in range(TOPK):
                dve.tensor_tensor(onehot[:, :, k], iota[:].unsqueeze(1).to_broadcast([P, NT, E]), idxf[:, :, k:k + 1].to_broadcast([P, NT, E]),
                                  ALU.is_equal).then_inc(s.onehot, 1)
            dve.wait_ge(s.onehot, TOPK)
            dve.tensor_reduce(picked[:], onehot[:].rearrange("p t k e -> p t e k"), AX.X, ALU.add).then_inc(s.picked, 1)
            dve.wait_ge(s.picked, 1)
            dve.tensor_tensor(wsel[:], picked[:], sig[:], ALU.mult).then_inc(s.wsel, 1)
            dve.wait_ge(s.wsel, 1)
            dve.tensor_reduce(wsum[:], wsel[:], AX.X, ALU.add).then_inc(s.wsum, 1)
            dve.wait_ge(s.wsum, 1)
            dve.reciprocal(wsum[:], wsum[:]).then_inc(s.wsum, 1)
            dve.wait_ge(s.wsum, 2)
            dve.tensor_tensor(cw[:, :, 0:E], wsel[:], wsum[:].unsqueeze(2).to_broadcast([P, NT, E]), ALU.mult).then_inc(s.cw, 1)
            dve.memset(cw[:, :, E:NE], 1.0).then_inc(s.cw, 1)
            dve.wait_ge(s.cw, 2)


def ffn(nc, a, out, mod_rows, x1, h2h, h2l, cw, w, ident):
    with ExitStack() as ctx:
        def sb(name, shape, dt=F32):
            return ctx.enter_context(nc.sbuf_tensor(name, shape, dt))

        def sem(name):
            return ctx.enter_context(nc.semaphore(name))

        silu = sb("silu", [P, 2, INTER])
        hid = sb("hid", [P, 4, HW])
        hth = sb("f_hth", [P, 2, 2, P], F32R)
        htl = sb("f_htl", [P, 2, 2, P], F32R)
        mod = sb("f_mod", [P, B, HID])
        y = sb("y", [P, NT, HID])

        up = ctx.enter_context(nc.psum_tensor("up", [P, 4, 512], F32))
        ht_ps = ctx.enter_context(nc.psum_tensor("ht_ps", [P, 2, 512], F32))
        y_ps = ctx.enter_context(nc.psum_tensor("y_ps", [P, 2, 512], F32))
        s = named({n: sem("f_" + n) for n in (
            "mod_in up silu hid dup ht hth htl down summed yg yo stored").split()})
        block = ctx.enter_context(nc.Block())

        PAIR = 2 * UNITS

        def stream(eng, step, lag):
            for k in range(PAIR):
                step(0, k)
            with eng.Fori(1, NG_E // 2) as i:
                for k in range(PAIR):
                    step(i, k)
            for k in range(lag):
                step(NG_E // 2, k)

        def unit(i, k):
            return i * PAIR + k

        def there(i, k):
            return not isinstance(i, int) or 0 <= unit(i, k) < NG_E * UNITS

        def where(k):
            k %= PAIR
            return k % UNITS // GE, k // UNITS * GE + k % GE

        @block.sync
        def _(sp):
            for b in range(B):
                sp.dma_start(mod[:, b], mod_rows[b:b + 1, 3].to_broadcast([P, HID])).then_inc(s.mod_in, 16)
            with sp.Fori(SLOTS + 1, NE) as e:
                load_expert(sp, a, w, e)
            for b in range(B):
                sp.wait_ge(s.yo, b + 1)
                sp.dma_start(out[b * QT:(b + 1) * QT].rearrange("t p h -> p t h"), y[:, b * QT:(b + 1) * QT]).then_inc(s.stored, 16)
            sp.wait_ge(s.stored, 16 * B)

        @block.gpsimd
        def _(pool):
            with pool.Fori(1, NG_E // 2) as i:
                for j in range(SLOTS):
                    pool.wait_ge(s.down, i * (2 * UNITS) + (j // GE - 1) * UNITS)
                    pool.tensor_tensor(w.tick[:, 2:3], w.tick_src[:], w.tick_src[:], ALU.mult)
                    split_expert(pool, w, i * SLOTS + j, j)
            pool.wait_ge(s.mod_in, 16 * B)
            for b in range(B):
                y_b = y[:, b * QT:(b + 1) * QT]
                pool.wait_ge(s.summed, (NG_E - 1) * NT + (b + 1) * QT)
                pool.tensor_tensor(y_b, y_b, mod[:, b:b + 1].to_broadcast([P, QT, HID]), ALU.mult).then_inc(s.yg, 1)
                pool.wait_ge(s.yg, b + 1)
                pool.tensor_tensor(y_b, y_b, x1[:, b * QT:(b + 1) * QT], ALU.add).then_inc(s.yo, 1)

        @block.scalar
        def _(act):
            def gate(i, k):
                n = unit(i, k)
                act.wait_ge(s.up, n + 1)
                after(act, s.hid, n - 1)
                act.activation(silu[:, k % 2], up[:, k % 4, 0:INTER], ACT.Silu).then_inc(s.silu, 1)

            def high(i, k):
                n = unit(i, k)
                act.wait_ge(s.ht, n + 1)
                after(act, s.down, n - 1)
                act.activation(hth[:, k % 2].rearrange("p c q -> p (c q)"), ht_ps[:, k % 2, 0:2 * P], ACT.Copy).then_inc(s.hth, 1)

            def step(i, k):
                if there(i, k):
                    gate(i, k)
                if there(i, k - 2):
                    high(i, k - 2)

            stream(act, step, 2)

        @block.vector
        def _(dve):
            def hidden(i, k):
                n = unit(i, k)
                t, slot = where(k)
                weight = cw[:, t, bass.ds(i * SLOTS + slot, 1)]
                dve.wait_ge(s.silu, n + 1)
                after(dve, s.ht, n - 3)
                dve.scalar_tensor_tensor(out=hid[:, k % 4, 0:INTER], in0=silu[:, k % 2], scalar=weight,
                                         in1=up[:, k % 4, INTER:2 * INTER], op0=ALU.mult, op1=ALU.mult).then_inc(s.hid, 1)
                dve.wait_ge(s.hid, n + 1)
                dve.tensor_copy(hid[:, k % 4, INTER:HW], hid[:, k % 4, HA:INTER]).then_inc(s.dup, 1)

            def low(i, k):
                n = unit(i, k)
                dve.wait_ge(s.hth, n + 1)
                after(dve, s.down, n - 1)
                dve.tensor_tensor(htl[:, k % 2].rearrange("p c q -> p (c q)"), ht_ps[:, k % 2, 0:2 * P],
                                  hth[:, k % 2].rearrange("p c q -> p (c q)").bitcast(F32), ALU.subtract).then_inc(s.htl, 1)

            def collect(i, k):
                n = unit(i, k)
                """After the last unit of a tile in a group: its sum into y."""
                t, slot = where(k)
                dve.wait_ge(s.down, n + 1)
                if isinstance(i, int) and n < UNITS:
                    dve.tensor_copy(y[:, t], y_ps[:, t % 2, 0:HID]).then_inc(s.summed, 1)
                else:
                    dve.tensor_tensor(y[:, t], y_ps[:, t % 2, 0:HID], y[:, t], ALU.add).then_inc(s.summed, 1)

            def step(i, k):
                if there(i, k):
                    hidden(i, k)
                if there(i, k - 2):
                    low(i, k - 2)
                if there(i, k - 4) and (k - 4) % GE == GE - 1:
                    collect(i, k - 4)

            stream(dve, step, 4)

        @block.tensor
        def _(pe):
            def up_mm(i, k):
                n = unit(i, k)
                t, slot = where(k)
                if t == 0:
                    pe.wait_ge(w.low_done, (i * SLOTS + slot) * 4 + 4)
                after(pe, s.hid, n - 3)
                o = up[:, k % 4, 0:2 * INTER]
                q = slice(t % QT * P, (t % QT + 1) * P)
                for c in range(KC):
                    xh, xl = h2h[:, t // QT, c, q], h2l[:, t // QT, c, q]
                    pe.matmul(o, xh, w.w13h[:, slot, c], start=(c == 0), stop=False)
                    pe.matmul(o, xh, w.w13l[:, slot, c], start=False, stop=False)
                    mm = pe.matmul(o, xl, w.w13h[:, slot, c], start=False, stop=(c == KC - 1))
                mm.then_inc(s.up, 1)

            def turn(i, k):
                n = unit(i, k)
                pe.wait_ge(s.dup, n + 1)
                after(pe, s.htl, n - 1)
                pe.transpose(ht_ps[:, k % 2, 0:P], hid[:, k % 4, 0:P], ident[:])
                pe.transpose(ht_ps[:, k % 2, P:2 * P], hid[:, k % 4, HA:HW], ident[:]).then_inc(s.ht, 1)

            def down_mm(i, k):
                n = unit(i, k)
                t, slot = where(k)
                q = k % 2
                pe.wait_ge(s.htl, n + 1)
                first, last = k % GE == 0, k % GE == GE - 1
                if first:
                    after(pe, s.summed, i * (PAIR // GE) + k // GE - 1)
                o = y_ps[:, t % 2, 0:HID]
                pe.matmul(o, hth[0:HA, q, 0], w.w2ah[:, slot], start=first, stop=False)
                pe.matmul(o, hth[0:HA, q, 0], w.w2al[:, slot], start=False, stop=False)
                pe.matmul(o, htl[0:HA, q, 0], w.w2ah[:, slot], start=False, stop=False)
                pe.matmul(o, hth[:, q, 1], w.w2b[:, slot], start=False, stop=False)
                pe.matmul(o, htl[:, q, 1], w.w2b[:, slot], start=False, stop=last).then_inc(s.down, 1)

            def step(i, k):
                if there(i, k):
                    up_mm(i, k)
                if there(i, k - 2):
                    turn(i, k - 2)
                if there(i, k - 3):
                    down_mm(i, k - 3)

            stream(pe, step, 3)


def lay_out(i):
    f = {k: np.asarray(x) for k, x in i.items()}
    chunks = lambda w: np.ascontiguousarray(w.reshape(KC, P, -1).transpose(1, 0, 2))
    w1 = np.concatenate([f["L0_ffn_w1"], f["L0_ffn_sw1"].reshape(HID, SHARED, INTER).transpose(1, 0, 2)])
    w3 = np.concatenate([f["L0_ffn_w3"], f["L0_ffn_sw3"].reshape(HID, SHARED, INTER).transpose(1, 0, 2)])
    w2 = np.concatenate([f["L0_ffn_w2"], f["L0_ffn_sw2"].reshape(SHARED, INTER, HID)])
    w13 = np.concatenate([w1, w3], 2).reshape(NE, KC, P, 2 * INTER).transpose(0, 2, 1, 3).reshape(NE, P, KC * 2 * INTER)
    wqkv = np.concatenate([f["L0_attn_Wq"], f["L0_attn_Wk"], f["L0_attn_Wv"]]).T
    return {
        "x": f["L0_attn_hidden_states"],
        "ct": chunks(f["L0_c"].T),
        "wmod": chunks(f["L0_wmod"]),
        "wqkv": chunks(wqkv),
        "wo": chunks(f["L0_attn_Wo"].T),
        "wgate": chunks(f["L0_ffn_gate_w"].T),
        "bias": np.broadcast_to(f["L0_ffn_expert_bias"][None, :], (P, E)),
        "w13": w13,
        "w2a": w2[:, 0:HA],
        "w2b": np.concatenate([w2[:, HA:], w2[:, HA:]], 1),
        **constants(),
    }


def kernel(**inputs):
    import concourse.bacc as bacc
    from concourse.bass_utils import run_bass_kernel_spmd

    nc = bacc.Bacc("TRN2", target_bir_lowering=False, num_devices=1)
    arrays, args = {}, {}
    for name, x in lay_out(inputs).items():
        x = np.ascontiguousarray(x)
        arrays[f"in_{name}"] = x
        args[name] = nc.dram_tensor(f"in_{name}", x.shape, mybir.dt.from_np(x.dtype), kind="ExternalInput").ap()
    out = nc.dram_tensor("out", (NT, P, HID), F32, kind="ExternalOutput").ap()
    build(nc, args, out)
    r = run_bass_kernel_spmd(nc, [arrays], core_ids=[0])
    return r.results[0]["out"].reshape(B, S, HID)
```
